# Optimizing a Trainium2 kernel written in Bass

```python
import numpy as np
import jax
import jax.numpy as jnp

def _softmax(x, axis=-1):
    return jax.nn.softmax(x, axis=axis)

def _gelu(x):
    return jax.nn.gelu(x, approximate=True)

def _silu(x):
    return jax.nn.silu(x)

def _sigmoid(x):
    return jax.nn.sigmoid(x)

def _layernorm(x, axis=-1, eps=1e-05):
    m = jnp.mean(x, axis=axis, keepdims=True)
    v = jnp.var(x, axis=axis, keepdims=True)
    return (x - m) / jnp.sqrt(v + eps)

def _scatter_add(tgt, idx, src, axis=0):
    return tgt.at[idx].add(src)

def _segment_sum(src, seg, n):
    return jax.ops.segment_sum(src, seg, n)
kernel_name = 'mk_prb_d1_jaxref_r4_e77f19'

def setup_inputs(seed: int=0):
    np.random.seed(seed)
    _w = jnp.asarray

    def _L0_attn_setup():
        import jax, jax.numpy as jnp
        import numpy as np
        EMBED_DIM = 256
        NUM_HEADS = 16
        HEAD_DIM = EMBED_DIM // NUM_HEADS
        B, T = (2, 512)
        key = jax.random.key(seed)
        kx, kqkv, kout = jax.random.split(key, 3)
        x = jax.random.normal(kx, (B, T, EMBED_DIM), dtype=jnp.float32)
        bound = 1.0 / np.sqrt(EMBED_DIM)
        w_qkv = jax.random.uniform(kqkv, (EMBED_DIM, 3 * EMBED_DIM), dtype=jnp.float32, minval=-bound, maxval=bound)
        w_out = jax.random.uniform(kout, (EMBED_DIM, EMBED_DIM), dtype=jnp.float32, minval=-bound, maxval=bound)
        return {'x': x, 'w_qkv': w_qkv, 'w_out': w_out}
    _L0_attn_in = _L0_attn_setup()

    def _L0_ffn_setup():
        import jax, jax.numpy as jnp
        import numpy as np
        B, T, D, R, E = (32, 256, 256, 64, 8)
        key = jax.random.key(seed)
        ks = jax.random.split(key, 12)
        inp = {}
        inp['x'] = jax.random.normal(ks[0], (B, T, D), dtype=jnp.float32)
        inp['base_W'] = jax.random.normal(ks[1], (D, D), dtype=jnp.float32) * (1.0 / np.sqrt(D))
        inp['base_b'] = jax.random.normal(ks[2], (D,), dtype=jnp.float32) * 0.01
        inp['disc_mu'] = jax.random.normal(ks[3], (E, D), dtype=jnp.float32) * 0.5
        inp['disc_sigma'] = jax.random.uniform(ks[4], (E, D), dtype=jnp.float32, minval=0.5, maxval=1.5)
        inp['down_W'] = jax.random.normal(ks[5], (E, D, R), dtype=jnp.float32) * (1.0 / np.sqrt(D))
        inp['down_b'] = jax.random.normal(ks[6], (E, R), dtype=jnp.float32) * 0.01
        inp['up_W'] = jax.random.normal(ks[7], (E, R, D), dtype=jnp.float32) * (1.0 / np.sqrt(R))
        inp['up_b'] = jax.random.normal(ks[8], (E, D), dtype=jnp.float32) * 0.01
        inp['conv_W'] = jax.random.normal(ks[9], (E, D, D), dtype=jnp.float32) * 0.02
        inp['conv_b'] = jax.random.normal(ks[10], (E, D), dtype=jnp.float32) * 0.01
        return inp
    _L0_ffn_in = _L0_ffn_setup()
    _d = {'L0_attn_x': _L0_attn_in['x'], 'L0_attn_w_qkv': _L0_attn_in['w_qkv'], 'L0_attn_w_out': _L0_attn_in['w_out'], 'L0_ffn_base_W': _L0_ffn_in['base_W'], 'L0_ffn_base_b': _L0_ffn_in['base_b'], 'L0_ffn_disc_mu': _L0_ffn_in['disc_mu'], 'L0_ffn_disc_sigma': _L0_ffn_in['disc_sigma'], 'L0_ffn_down_W': _L0_ffn_in['down_W'], 'L0_ffn_down_b': _L0_ffn_in['down_b'], 'L0_ffn_up_W': _L0_ffn_in['up_W'], 'L0_ffn_up_b': _L0_ffn_in['up_b'], 'L0_ffn_conv_W': _L0_ffn_in['conv_W'], 'L0_ffn_conv_b': _L0_ffn_in['conv_b']}
    _x0 = _d['L0_attn_x']
    _d['L0_attn_x'] = jax.random.normal(jax.random.fold_in(jax.random.key(seed), 1), (1, 4096, 256), dtype=_x0.dtype)
    del _x0
    return _d

def reference(L0_attn_x, L0_attn_w_qkv, L0_attn_w_out, L0_ffn_base_W, L0_ffn_base_b, L0_ffn_disc_mu, L0_ffn_disc_sigma, L0_ffn_down_W, L0_ffn_down_b, L0_ffn_up_W, L0_ffn_up_b, L0_ffn_conv_W, L0_ffn_conv_b):

    def _L0_attn_ref(x, w_qkv, w_out):
        import jax, jax.numpy as jnp
        import numpy as np
        EMBED_DIM = 256
        NUM_HEADS = 16
        HEAD_DIM = EMBED_DIM // NUM_HEADS
        B, T = (2, 512)
        Bx, Tx, C = x.shape
        qkv = x @ w_qkv
        q, k, v = jnp.split(qkv, 3, axis=-1)

        def split_heads(t):
            return t.reshape(Bx, Tx, NUM_HEADS, HEAD_DIM).transpose(0, 2, 1, 3)
        q, k, v = (split_heads(q), split_heads(k), split_heads(v))
        scale = 1.0 / jnp.sqrt(jnp.float32(HEAD_DIM))
        scores = jnp.einsum('bhqd,bhkd->bhqk', q, k) * scale
        causal = jnp.tril(jnp.ones((Tx, Tx), dtype=bool))
        scores = jnp.where(causal, scores, jnp.float32(-jnp.inf))
        weights = jax.nn.softmax(scores, axis=-1)
        out = jnp.einsum('bhqk,bhkd->bhqd', weights, v)
        out = out.transpose(0, 2, 1, 3).reshape(Bx, Tx, C)
        return out @ w_out

    def _L0_ffn_ref(x, base_W, base_b, disc_mu, disc_sigma, down_W, down_b, up_W, up_b, conv_W, conv_b):
        import jax, jax.numpy as jnp
        import numpy as np
        B, T, D, R, E = (32, 256, 256, 64, 8)
        base = jnp.einsum('btd,od->bto', x, base_W) + base_b
        m1 = x.mean(axis=1)
        m2 = (x * x).mean(axis=1)
        inv_var = 1.0 / (disc_sigma * disc_sigma)
        losses = (jnp.einsum('bd,ed->eb', m2, inv_var) - 2.0 * jnp.einsum('bd,ed->eb', m1, disc_mu * inv_var) + jnp.sum(disc_mu * disc_mu * inv_var, axis=1)[:, None]) / D
        idx = jnp.argmin(losses, axis=0)
        Wd, bd = (down_W[idx], down_b[idx])
        Wu, bu = (up_W[idx], up_b[idx])
        Wc, bc = (conv_W[idx], conv_b[idx])
        h = jax.nn.relu(jnp.einsum('btd,bdr->btr', x, Wd) + bd[:, None, :])
        a = jnp.einsum('btr,brd->btd', h, Wu) + bu[:, None, :]
        y = jnp.einsum('btd,bod->bto', a, Wc) + bc[:, None, :]
        return base + y
    x = L0_attn_x
    xn = _layernorm(x, axis=-1)
    x = x + _L0_attn_ref(xn, L0_attn_w_qkv, L0_attn_w_out) + _L0_ffn_ref(xn, L0_ffn_base_W, L0_ffn_base_b, L0_ffn_disc_mu, L0_ffn_disc_sigma, L0_ffn_down_W, L0_ffn_down_b, L0_ffn_up_W, L0_ffn_up_b, L0_ffn_conv_W, L0_ffn_conv_b)
    return x

_drawn_inputs = setup_inputs


def setup_inputs(seed=0):
    import zlib

    import numpy as np

    out = dict(_drawn_inputs(seed))
    spreads = {}
    factors = {'L0_attn_w_qkv': 4.749,
     'L0_attn_w_out': 4.699,
     'L0_ffn_base_b': 31.832,
     'L0_ffn_down_b': 177.226,
     'L0_ffn_up_b': 64.0,
     'L0_ffn_conv_b': 33.527}
    for name, (base, spread) in spreads.items():
        noise = np.random.default_rng([zlib.crc32(name.encode()), seed]).standard_normal(out[name].shape)
        drawn = base * np.exp(spread * noise) if base else spread * noise
        out[name] = jnp.asarray(drawn.astype(out[name].dtype))
    for name, factor in factors.items():
        out[name] = (out[name] * factor).astype(out[name].dtype)
    return out
```

```python
import concourse.bass as bass
from concourse import mybir
from contextlib import ExitStack

F32 = mybir.dt.float32
BF16 = mybir.dt.bfloat16
U32 = mybir.dt.uint32
ACT = mybir.ActivationFunctionType
ALU = mybir.AluOpType
AX = mybir.AxisListType

T = 4096
C = 256
HEADS = 16
D = C // HEADS
E = 8
R = 64
P = 128
CH = 512
NCH = T // CH
NT = CH // P
J = 4
NG = HEADS // J
EPS = 1e-5
NEG = -3.0e38
SCALE = 0.25

PRODUCTS = [(0, 0), (0, 1), (1, 0), (1, 1), (0, 2), (2, 0)]
SK = D * len(PRODUCTS)
MR = 3 * J
SM = SK + MR

DMA = 16


def micro(qc, g, pos=0):
    return 2 * NT * qc * (qc + 1) + g * (NT * (qc + 1)) + pos


def item(qc, g):
    return NG * qc + g


def wait(eng, sem, value):
    if not isinstance(value, int) or value > 0:
        eng.wait_ge(sem, value)


def wait_apart(eng, sem, value, true_sem, true_value):
    wait(eng, sem, value)
    eng.wait_ge(true_sem, true_value)


def layernorm_projections(nc, io, scratch):
    parts_d, v_d, rest_d = scratch
    with ExitStack() as ctx:
        def sb(name, shape, dt=F32):
            return ctx.enter_context(nc.sbuf_tensor(name, shape, dt))

        def sem(name):
            return ctx.enter_context(nc.semaphore(name))

        x_sb = sb("x_sb", [P, NCH * NT, C])
        xn = sb("xn", [P, 2, NT, C])
        xs = sb("xs", [P, 2, 2, CH])
        xnT = sb("xnT", [P, 2, T])
        wqkv = sb("wqkv", [P, 2, 3 * C])
        wbase = sb("wbase", [P, 2, C])
        ident = sb("ident", [P, P])
        stats = sb("stats", [P, NT, 6])
        mv = sb("mv", [P, NT, 2])
        var = sb("var", [P, NT])
        std = sb("std", [P, NT])
        rs = sb("rs", [P, NT])
        tq = sb("tq", [P, NT])
        ts2 = sb("ts2", [P, NT])
        th = sb("th", [P, NT])
        rstd = sb("rstd", [P, NT])
        sum1 = sb("sum1", [P, 2, NCH])
        sum2 = sb("sum2", [P, 2, NCH])
        junk = sb("junk", [P, 2, CH], BF16)
        stage = sb("stage", [P, 4, 3, CH], BF16)
        rest1 = sb("rest1", [P, 2, CH])
        vst = sb("vst", [P, 2, NG, NT, J * D])
        muT = sb("muT", [P, 2, E])
        sgT = sb("sgT", [P, 2, E])
        sq = sb("sq", [P, 2, E])
        iv = sb("iv", [P, 2, E])
        miv = sb("miv", [P, 2, E])
        m2iv = sb("m2iv", [P, 2, E])
        mmiv = sb("mmiv", [P, 2, E])
        ones = sb("ones", [P, 1])
        m1 = sb("m1", [P, 2])
        m2 = sb("m2", [P, 2])
        m1s = sb("m1s", [P, 2])
        m2s = sb("m2s", [P, 2])
        nloss = sb("nloss", [1, E])
        best = sb("best", [1, 8])
        index = sb("index", [1, 8], U32)
        wdown = sb("wdown", [P, 2, R])
        bdown = sb("bdown", [R, 1])
        wup = sb("wup", [P, 2, R + 1])
        wconv = sb("wconv", [P, 2, C])
        brow = sb("brow", [R + 1, C])
        bbase = sb("bbase", [R + 1, C])
        wuc0 = sb("wuc0", [R + 1, C])
        wuc = sb("wuc", [R + 1, C])
        hT = sb("hT", [R + 1, 2, CH])

        tp = ctx.enter_context(nc.psum_tensor("tp", [P, 2, CH], F32))
        qk_ps = ctx.enter_context(nc.psum_tensor("qk_ps", [P, 2, CH], F32))
        vb_ps = ctx.enter_context(nc.psum_tensor("vb_ps", [P, 4, CH], F32))

        x_in = [sem(f"x_in{n}") for n in range(2)]
        w_in = sem("w_in")
        ln_step = sem("ln_step")
        var_ready = sem("var_ready")
        std_ready = sem("std_ready")
        xn_ready = sem("xn_ready")
        tp_ready = sem("tp_ready")
        tp_copied = sem("tp_copied")
        tp_squared = sem("tp_squared")
        qk_ready = sem("qk_ready")
        part1_ready = sem("part1_ready")
        rest_ready = sem("rest_ready")
        part2_ready = sem("part2_ready")
        part3_ready = sem("part3_ready")
        parts_out = [sem(f"parts_out{n}") for n in range(4)]
        v_psum = sem("v_psum")
        v_staged = sem("v_staged")
        v_out = [sem(f"v_out{n}") for n in range(2)]
        base_ready = sem("base_ready")
        base_added = sem("base_added")
        set_up = sem("set_up")
        xnT_ready = sem("xnT_ready")
        mean_ready = sem("mean_ready")
        loss_step = sem("loss_step")
        loss_ready = sem("loss_ready")
        index_ready = sem("index_ready")
        expert_in = sem("expert_in")
        wuc_psum = sem("wuc_psum")
        wuc_ready = sem("wuc_ready")
        h_psum = sem("h_psum")
        h_ready = sem("h_ready")
        ffn_ready = sem("ffn_ready")
        ffn_added = sem("ffn_added")
        rest_out = sem("rest_out")
        block = ctx.enter_context(nc.Block())

        def chunks(eng, body, peeled=False):
            if peeled:
                for c in range(NCH):
                    body(c, c % 2)
                return
            body(0, 0)
            body(1, 1)
            with eng.Fori(1, NCH // 2) as pair:
                body(pair * 2, 0)
                body(pair * 2 + 1, 1)

        def x_rows(c):
            return io["x"][c * CH:(c + 1) * CH, :].rearrange("(t p) n -> p t n", p=P)

        W_COUNT = 8

        @block.sync
        def _(sp):
            for c in range(NCH):
                wait(sp, x_in[c % 2], DMA * (c // 2))
                sp.dma_start(x_sb[:, c * NT:(c + 1) * NT, :], x_rows(c)).then_inc(x_in[c % 2], DMA)

            def store(c, par):
                for u in range(4):
                    sp.wait_ge(part3_ready, c * 4 + (u + 1))
                    sp.dma_start(
                        parts_d[(u // 2) * 3 * C:(u // 2 + 1) * 3 * C, bass.ds(c * CH, CH)]
                        .rearrange("(s n) t -> n s t", s=3)[(u % 2) * P:(u % 2 + 1) * P],
                        stage[:, u, :, :]).then_inc(parts_out[u], DMA)
                sp.wait_ge(v_staged, c * NT + NT)
                sp.dma_start(v_d.rearrange("(g p) n -> p g n", p=P)[:, :, bass.ds(c * 256, 256)],
                             vst[:, par, :, :, :].rearrange("p g t n -> p g (t n)")).then_inc(v_out[par], DMA)

            chunks(sp, store)
            sp.wait_ge(index_ready, 1)
            expert = sp.value_load(index[0:1, 0:1], min_val=0, max_val=E - 1)
            sp.dma_start(wdown[:, :, :].rearrange("p a b -> p (a b)"),
                         io["down_W"][bass.ds(expert * P, P), :]).then_inc(expert_in, DMA)
            sp.dma_start(bdown[:, :], io["down_b"][bass.ds(expert * R, R), :]).then_inc(expert_in, DMA)
            sp.dma_start(wup[:, :, :].rearrange("p a b -> p (a b)"),
                         io["up_W"][bass.ds(expert * P, P), :]).then_inc(expert_in, DMA)
            sp.dma_start(wconv[:, :, :].rearrange("p a b -> p (a b)"),
                         io["conv_W"][bass.ds(expert * P, P), :]).then_inc(expert_in, DMA)
            sp.dma_start(brow[R:R + 1, :], io["conv_b"][bass.ds(expert, 1), :]).then_inc(expert_in, DMA)

            def store_rest(c, par):
                sp.wait_ge(ffn_added, c * NT + NT)
                sp.dma_start(rest_d[bass.ds(c * CH, CH), :].rearrange("(t p) n -> p t n", p=P),
                             x_sb[:, bass.ds(c * NT, NT), :]).then_inc(rest_out, DMA)

            chunks(sp, store_rest)
            for u in range(4):
                sp.wait_ge(parts_out[u], DMA * NCH)
            for n in range(2):
                sp.wait_ge(v_out[n], DMA * NCH // 2)
            sp.wait_ge(rest_out, DMA * NCH)

        @block.scalar
        def _(act):
            act.dma_start(ident[:, :], io["identity"]).then_inc(w_in, DMA)
            act.dma_start(wqkv[:, :, :], io["w_qkv"].rearrange("(a p) n -> p a n", p=P)).then_inc(w_in, DMA)
            act.dma_start(wbase[:, :, :], io["base_W"].rearrange("(a p) n -> p a n", p=P)).then_inc(w_in, DMA)
            act.dma_start(muT[:, :, :], io["disc_mu"].rearrange("(a p) n -> p a n", p=P)).then_inc(w_in, DMA)
            act.dma_start(sgT[:, :, :], io["disc_sigma"].rearrange("(a p) n -> p a n", p=P)).then_inc(w_in, DMA)
            act.wait_ge(set_up, 1)
            act.dma_start(bbase[R:R + 1, :], io["base_b"]).then_inc(w_in, DMA)

            def body(c, par):
                act.wait_ge(var_ready, c + 1)
                nc.scalar.activation(std[:, :], var[:, :], ACT.Sqrt).then_inc(std_ready, 1)
                for h in range(2):
                    act.wait_ge(tp_ready, c * 2 + (h + 1))
                    if not isinstance(c, int) or c >= 2:
                        act.wait_ge(base_ready, (c - 1) * NT)
                        act.wait_ge(xnT_ready, c - 1)
                    nc.scalar.activation(xs[:, par, h, :], tp[:, h, :], ACT.Copy,
                                         accum_out=sum1[:, h, bass.ds(c, 1)]).then_inc(tp_copied, 1)
                    wait(act, tp_squared, c * 2 + (h - 1))
                    nc.scalar.activation(junk[:, h, :], tp[:, h, :], ACT.Square,
                                         accum_out=sum2[:, h, bass.ds(c, 1)]).then_inc(tp_squared, 1)
                for u in range(4):
                    act.wait_ge(qk_ready, c * 4 + (u + 1))
                    wait(act, parts_out[u], c * DMA)
                    nc.scalar.activation(stage[:, u, 0, :], qk_ps[:, u % 2, :], ACT.Copy).then_inc(part1_ready, 1)
                for t in range(NT):
                    act.wait_ge(v_psum, c * NT + (t + 1))
                    if t == 0 and (not isinstance(c, int) or c >= 2):
                        act.wait_ge(v_out[par], (c - par) * (DMA // 2))
                    nc.scalar.activation(vst[:, par, :, t, :],
                                         vb_ps[:, t % 2, 0:C].rearrange("p (g n) -> p g n", g=NG),
                                         ACT.Copy).then_inc(v_staged, 1)

            chunks(act, body)

        @block.gpsimd
        def _(pool):
            def body(c, par):
                pool.wait_ge(tp_copied, c * 2 + 2)
                nc.gpsimd.tensor_copy(xnT[:, :, bass.ds(c * CH, CH)], xs[:, par, :, :]).then_inc(xnT_ready, 1)
                for u in range(4):
                    n = c * 4 + u
                    pool.wait_ge(rest_ready, n + 1)
                    wait(pool, parts_out[u], c * DMA)
                    nc.gpsimd.tensor_copy(stage[:, u, 1, :], rest1[:, u % 2, :]).then_inc(part2_ready, 1)
                    pool.wait_ge(part2_ready, n + 1)
                    nc.gpsimd.tensor_tensor(stage[:, u, 2, :], rest1[:, u % 2, :], stage[:, u, 1, :],
                                            ALU.subtract).then_inc(part3_ready, 1)

            chunks(pool, body, peeled=True)

        @block.vector
        def _(dve):
            v = nc.vector
            v.memset(brow[:, :], 0.0)
            v.memset(ones[:, :], 1.0)
            v.memset(hT[R:R + 1, :, :], 1.0)
            v.memset(bbase[:, :], 0.0).then_inc(set_up, 1)
            dve.wait_ge(w_in, DMA * 6)

            LN_STEPS = 7

            def body(c, par):
                step = [0]

                def link(ins):
                    step[0] += 1
                    ins.then_inc(ln_step, 1)
                    dve.wait_ge(ln_step, c * LN_STEPS + step[0])

                dve.wait_ge(x_in[par], (c - par) * (DMA // 2) + DMA)
                wait(dve, xn_ready, c)
                for t in range(NT):
                    last = v.bn_stats(stats[:, t, :], x_sb[:, bass.ds(c * NT + t, 1), :]
                                      .rearrange("p a n -> p (a n)"))
                link(last)
                for t in range(NT):
                    last = v.bn_aggr(mv[:, t, :], stats[:, t, :])
                link(last)
                v.tensor_scalar(var[:, :], mv[:, :, 1], EPS, None, ALU.add).then_inc(var_ready, 1)
                dve.wait_ge(std_ready, c + 1)
                link(v.reciprocal(rs[:, :], std[:, :]))
                link(v.tensor_tensor(tq[:, :], var[:, :], rs[:, :], ALU.mult))
                link(v.tensor_tensor(ts2[:, :], tq[:, :], std[:, :], ALU.add))
                link(v.tensor_scalar(th[:, :], ts2[:, :], 0.5, None, ALU.mult))
                link(v.reciprocal(rstd[:, :], th[:, :]))
                assert step[0] == LN_STEPS
                if not isinstance(c, int) or c >= 2:
                    dve.wait_ge(tp_ready, (c - 1) * 2)
                for t in range(NT):
                    last = v.tensor_scalar(xn[:, par, t, :], x_sb[:, bass.ds(c * NT + t, 1), :]
                                           .rearrange("p a n -> p (a n)"),
                                           mv[:, t, 0:1], rstd[:, t:t + 1], ALU.subtract, ALU.mult)
                last.then_inc(xn_ready, 1)
                for u in range(4):
                    n = c * 4 + u
                    dve.wait_ge(part1_ready, n + 1)
                    wait(dve, part3_ready, n - 1)
                    v.tensor_tensor(rest1[:, u % 2, :], qk_ps[:, u % 2, :], stage[:, u, 0, :],
                                    ALU.subtract).then_inc(rest_ready, 1)
                for t in range(NT):
                    dve.wait_ge(base_ready, c * NT + (t + 1))
                    xt = x_sb[:, bass.ds(c * NT + t, 1), :].rearrange("p a n -> p (a n)")
                    v.tensor_tensor(xt, vb_ps[:, 2 + t % 2, 0:C], xt, ALU.add).then_inc(base_added, 1)

            chunks(dve, body, peeled=True)

            done = [0]

            def link(ins):
                done[0] += 1
                ins.then_inc(loss_step, 1)
                dve.wait_ge(loss_step, done[0])

            link(v.tensor_tensor(sq[:, :, :], sgT[:, :, :], sgT[:, :, :], ALU.mult))
            link(v.reciprocal(iv[:, :, :], sq[:, :, :]))
            link(v.tensor_tensor(miv[:, :, :], muT[:, :, :], iv[:, :, :], ALU.mult))
            link(v.tensor_scalar(m2iv[:, :, :], miv[:, :, :], -2.0, None, ALU.mult))
            link(v.tensor_tensor(mmiv[:, :, :], miv[:, :, :], muT[:, :, :], ALU.mult))
            dve.wait_ge(tp_squared, 2 * NCH)
            link(v.tensor_reduce(out=m1s[:, :], in_=sum1[:, :, :], axis=AX.X, op=ALU.add))
            link(v.tensor_reduce(out=m2s[:, :], in_=sum2[:, :, :], axis=AX.X, op=ALU.add))
            link(v.tensor_scalar(m1[:, :], m1s[:, :], 1.0 / T, None, ALU.mult))
            v.tensor_scalar(m2[:, :], m2s[:, :], 1.0 / T, None, ALU.mult).then_inc(mean_ready, 1)
            dve.wait_ge(loss_ready, 1)
            link(v.tensor_scalar(nloss[:, :], tp[0:1, 0, 0:E], -1.0 / C, None, ALU.mult))
            link(v.max(best[:, :], nloss[:, :]))
            v.max_index(index[:, :], best[:, :], nloss[:, :]).then_inc(index_ready, 1)
            dve.wait_ge(wuc_psum, 1)
            link(v.tensor_tensor(wuc0[:, :], tp[0:R + 1, 1, 0:C], brow[:, :], ALU.add))
            v.tensor_tensor(wuc[:, :], wuc0[:, :], bbase[:, :], ALU.add).then_inc(wuc_ready, 1)

            def ffn(c, par):
                dve.wait_ge(h_psum, c + 1)
                if not isinstance(c, int) or c >= 2:
                    dve.wait_ge(ffn_ready, (c - 1) * NT)
                v.tensor_scalar(hT[0:R, par, :], qk_ps[0:R, par, :], bdown[:, 0:1], 0.0,
                                ALU.add, ALU.max).then_inc(h_ready, 1)
                for t in range(NT):
                    dve.wait_ge(ffn_ready, c * NT + (t + 1))
                    xt = x_sb[:, bass.ds(c * NT + t, 1), :].rearrange("p a n -> p (a n)")
                    v.tensor_tensor(xt, vb_ps[:, t, 0:C], xt, ALU.add).then_inc(ffn_added, 1)

            dve.wait_ge(base_added, NT * NCH)
            chunks(dve, ffn, peeled=True)

        @block.tensor
        def _(pe):
            pe.wait_ge(w_in, DMA * 6)

            def body(c, par):
                pe.wait_ge(xn_ready, c + 1)
                for h in range(2):
                    wait(pe, tp_squared, c * 2 - 1 + h)
                    for t in range(NT):
                        last = nc.tensor.transpose(tp[:, h, t * P:(t + 1) * P],
                                                   xn[:, par, t, h * P:(h + 1) * P], ident[:, :])
                    last.then_inc(tp_ready, 1)
                pe.wait_ge(tp_copied, c * 2 + 2)
                for u in range(4):
                    n = c * 4 + u
                    wait(pe, rest_ready, n - 1)
                    for h in range(2):
                        last = nc.tensor.matmul(qk_ps[:, u % 2, :], wqkv[:, h, u * P:(u + 1) * P],
                                                xs[:, par, h, :], start=(h == 0), stop=(h == 1))
                    last.then_inc(qk_ready, 1)
                for t in range(NT):
                    wait(pe, v_staged, c * NT + (t - 1))
                    for h in range(2):
                        last = nc.tensor.matmul(vb_ps[:, t % 2, 0:C], xs[:, par, h, t * P:(t + 1) * P],
                                                wqkv[:, h, 2 * C:3 * C], start=(h == 0), stop=(h == 1))
                    last.then_inc(v_psum, 1)
                    wait(pe, base_added, c * NT + (t - 1))
                    for h in range(2):
                        last = nc.tensor.matmul(vb_ps[:, 2 + t % 2, 0:C], xs[:, par, h, t * P:(t + 1) * P],
                                                wbase[:, h, :], start=(h == 0), stop=(h == 1))
                    last.then_inc(base_ready, 1)

            chunks(pe, body)
            pe.wait_ge(mean_ready, 1)
            terms = [(m2[:, h:h + 1], iv[:, h, :]) for h in range(2)]
            terms += [(m1[:, h:h + 1], m2iv[:, h, :]) for h in range(2)]
            terms += [(ones[:, :], mmiv[:, h, :]) for h in range(2)]
            for n, (a, b) in enumerate(terms):
                last = nc.tensor.matmul(tp[0:1, 0, 0:E], a, b, start=(n == 0), stop=(n == len(terms) - 1))
            last.then_inc(loss_ready, 1)
            pe.wait_ge(expert_in, DMA * 5)
            for h in range(2):
                last = nc.tensor.matmul(tp[0:R + 1, 1, 0:C], wup[:, h, :], wconv[:, h, :],
                                        start=(h == 0), stop=(h == 1))
            last.then_inc(wuc_psum, 1)
            pe.wait_ge(xnT_ready, NCH)
            pe.wait_ge(v_staged, NCH * NT)
            pe.wait_ge(base_added, NCH * NT)
            pe.wait_ge(rest_ready, NCH * 4)
            pe.wait_ge(wuc_ready, 1)

            def ffn(c, par):
                wait(pe, h_ready, c - 1)
                for h in range(2):
                    last = nc.tensor.matmul(qk_ps[0:R, par, :], wdown[:, h, :],
                                            xnT[:, h, bass.ds(c * CH, CH)], start=(h == 0), stop=(h == 1))
                last.then_inc(h_psum, 1)
                pe.wait_ge(h_ready, c + 1)
                for t in range(NT):
                    wait(pe, ffn_added, c * NT + (t - 3))
                    nc.tensor.matmul(vb_ps[:, t, 0:C], hT[:, par, t * P:(t + 1) * P], wuc[:, :],
                                     start=True, stop=True).then_inc(ffn_ready, 1)

            chunks(pe, ffn)


def attention(nc, io, scratch, out):
    parts_d, v_d, rest_d = scratch
    with ExitStack() as ctx:
        def sb(name, shape, dt=F32):
            return ctx.enter_context(nc.sbuf_tensor(name, shape, dt))

        def sem(name):
            return ctx.enter_context(nc.semaphore(name))

        k_st = sb("k_st", [P, HEADS * T], BF16)
        q_st = sb("q_st", [P, NG * J * CH], BF16)
        v_buf = sb("v_buf", [P, 2 * NCH * NT * J * D])
        v_ring = sb("v_ring", [P, NT, J, 32])
        probs = sb("probs", [P, 2, J, CH])
        on = sb("on", [P, (NG + 1) * CH])
        o_t = sb("o_t", [P, CH])
        l_rec = sb("l_rec", [P, CH // 32])
        rest = sb("rest", [P, NT, C])
        w_out = sb("w_out", [P, NG, C])
        ident = sb("ident_b", [P, P], BF16)
        mask = sb("mask", [P, CH], BF16)
        masked = sb("masked", [P, 2, CH], BF16)
        maxes = sb("maxes", [P, NCH + 1, NT * J])
        negmax = sb("negmax", [P, NT * J])
        negrest = sb("negrest", [P, NT * J])
        mparts = sb("mparts", [P, NT, P], BF16)

        s1 = ctx.enter_context(nc.psum_tensor("s1", [P, 4, CH], F32))
        s2 = ctx.enter_context(nc.psum_tensor("s2", [P, 2, CH], F32))
        acc = ctx.enter_context(nc.psum_tensor("acc", [P, CH], F32))
        mt_ps = ctx.enter_context(nc.psum_tensor("mt_ps", [P, 2 * CH], BF16))

        const_in = sem("const_in")
        set_up = sem("set_up2")
        k_in = sem("k_in")
        q_in = sem("q_in")
        v_in = sem("v_in")
        rest_in = sem("rest_in")
        s1_ready = sem("s1_ready")
        s1_read = sem("s1_read")
        split_step = sem("split_step")
        m_ready = sem("m_ready")
        mt_ready = sem("mt_ready")
        m_placed = sem("m_placed")
        s2_ready = sem("s2_ready")
        exp_done = sem("exp_done")
        mask_done = sem("mask_done")
        v_ready = sem("v_ready")
        av_done = sem("av_done")
        acc_read = sem("acc_read")
        l_ready = sem("l_ready")
        scaled = sem("scaled")
        on_ready = sem("on_ready")
        proj_ready = sem("proj_ready")
        proj_added = sem("proj_added")
        out_done = sem("out_done")
        block = ctx.enter_context(nc.Block())

        SPLIT_STEPS = 4

        def k_at(g, j, at, n):
            return bass.ds((g * J + j) * T + at, n)

        def items(eng, body, between, peeled=False):
            for qc in range(NCH):
                for half in range(2):
                    if peeled or qc in (0, 1, NCH - 1):
                        for gg in range(2):
                            body(qc, 2 * half + gg, half, gg)
                    else:
                        with eng.Fori(0, 2) as gg:
                            body(qc, gg + 2 * half, half, gg)
                    if half == 0:
                        between(qc)

        def full_chunks(eng, count, body):
            if count == 1:
                body(0)
            elif count > 1:
                with eng.Fori(0, count) as kc:
                    body(kc)

        def ahead(qc, half, gg):
            if half == 0:
                return qc, gg + 2
            return (qc + 1, gg) if qc + 1 < NCH else None

        @block.sync
        def _(sp):
            sp.dma_start(ident[:, :], io["identity_b"]).then_inc(const_in, DMA)
            sp.dma_start(mask[:, :], io["mask"]).then_inc(const_in, DMA)
            sp.dma_start(w_out[:, :, :], io["w_out"].rearrange("(g p) n -> p g n", p=P)).then_inc(const_in, DMA)

            def load_k(c):
                wait(sp, k_in, c * DMA * (len(PRODUCTS) + 1))
                kv = k_st[:, :].rearrange("p (h t) -> p h t", h=HEADS)[:, :, c * CH:(c + 1) * CH]
                for n, (_, part) in enumerate(PRODUCTS):
                    src = parts_d[(3 + part) * C:(4 + part) * C, c * CH:(c + 1) * CH]
                    sp.dma_start(kv[n * D:(n + 1) * D], src.rearrange("(h d) t -> d h t", d=D)).then_inc(k_in, DMA)
                sp.dma_start(kv[SK:SM], io["head_rows"].rearrange("r (h t) -> r h t", h=HEADS)).then_inc(k_in, DMA)

            def load_q(n, qc, g, free):
                wait(sp, q_in, n * (DMA * len(PRODUCTS)))
                wait(sp, s2_ready, free)
                for r, (part, _) in enumerate(PRODUCTS):
                    src = parts_d[bass.ds(part * C + g * (J * D), J * D), bass.ds(qc * CH, CH)]
                    sp.dma_start(q_st[r * D:(r + 1) * D, bass.ds(g * (J * CH), J * CH)]
                                 .rearrange("p (j t) -> p j t", j=J),
                                 src.rearrange("(j d) t -> d j t", d=D)).then_inc(q_in, DMA)

            def load_v(n, g, slot, count, free):
                wait(sp, v_in, n * DMA)
                wait(sp, v_ready, free)
                sp.dma_start(v_buf[:, bass.ds(slot * (NCH * 256), count * 256)],
                             v_d[bass.ds(g * P, P), 0:count * 256]).then_inc(v_in, DMA)

            load_k(0)
            for g in range(3):
                load_q(g, 0, g, 0)
            load_v(0, 0, 0, 1, 0)
            load_k(1)

            def body(qc, g, half, gg):
                now = micro(qc, g)
                if half == 0:
                    if not (qc == NCH - 1 and gg == 1):
                        load_q(item(qc, g) + 3, gg + qc, gg * -3 + 3, now * 4)
                elif qc + 1 < NCH:
                    load_q(item(qc, g) + 3, qc + 1, gg + 1, now * 4)
                last = isinstance(g, int) and item(qc, g) == NCH * NG - 1
                if not last:
                    load_v(item(qc, g) + 1, gg + 1 if half == 0 else gg * -3 + 3, gg * -1 + 1,
                           min(NCH, qc + 2), now)

            def load_rest(c):
                wait(sp, out_done, c * NT * DMA)
                sp.dma_start(rest[:, :, :], rest_d[c * CH:(c + 1) * CH, :]
                             .rearrange("(t p) n -> p t n", p=P)).then_inc(rest_in, DMA)

            def store(c):
                for t in range(NT):
                    sp.wait_ge(proj_added, c * NT + t + 1)
                    sp.dma_start(out[c * CH + t * P:c * CH + (t + 1) * P, :],
                                 rest[:, t, :]).then_inc(out_done, DMA)

            def between(qc):
                if qc + 2 < NCH:
                    load_k(qc + 2)
                if qc > 0:
                    load_rest(qc - 1)
                    store(qc - 1)

            items(sp, body, between)
            load_rest(NCH - 1)
            store(NCH - 1)
            sp.wait_ge(out_done, NCH * NT * DMA)

        @block.tensor
        def _(pe):
            mm = nc.tensor.matmul

            def max_scores(qc, g, pos, kc, t, r):
                n = P * (t + 1) if kc is None else CH
                at = qc * CH if kc is None else kc * CH
                wait(pe, s1_read, micro(qc, g, pos) * 2 + (r - 1))
                for j in (2 * r, 2 * r + 1):
                    last = mm(s1[:, j, 0:n], q_st[0:SK, bass.ds(g * (J * CH) + (j * CH + t * P), P)],
                              k_st[0:SK, k_at(g, j, at, n)], start=True, stop=True)
                last.then_inc(s1_ready, 1)

            def scores(qc, g, pos, kc, i, j):
                q0 = i * P if kc is None else 0
                at = (qc if kc is None else kc) * CH + i * P
                wait(pe, exp_done, micro(qc, g, pos) * 4 + (j - 1))
                mm(s2[:, j % 2, q0:CH], k_st[0:SM, k_at(g, j, at, P)],
                   q_st[0:SM, bass.ds(g * (J * CH) + (j * CH + q0), CH - q0)],
                   start=True, stop=True).then_inc(s2_ready, 1)

            def weigh(mu, i, diagonal, masks, first, final, taken):
                q0 = i * P if diagonal else 0
                if diagonal:
                    pe.wait_ge(mask_done, masks)
                else:
                    pe.wait_ge(exp_done, mu * 4 + 4)
                pe.wait_ge(v_ready, mu + 1)
                if first:
                    wait(pe, acc_read, taken)
                for j in range(J):
                    last = mm(acc[32 * j:32 * j + 32, q0:CH], v_ring[:, i, j, :], probs[:, i % 2, j, q0:CH],
                              start=first, stop=final, tile_position=(0, 32 * j))
                last.then_inc(av_done, 1)

            def transpose_maxima(n):
                pe.wait_ge(m_ready, n + 1)
                wait(pe, m_placed, n)
                for t in range(NT):
                    last = nc.tensor.transpose(mt_ps[:, t * P:(t + 1) * P], mparts[:, t, :], ident[:, :])
                last.then_inc(mt_ready, 1)

            def step(now, mu, pos, kc, i, nxt, kn, pn, before):
                qc, g = now
                scores(qc, g, pos, kc, i, 0)
                scores(qc, g, pos, kc, i, 1)
                if nxt:
                    max_scores(*nxt, pn, kn, i, 0)
                    max_scores(*nxt, pn, kn, i, 1)
                scores(qc, g, pos, kc, i, 2)
                scores(qc, g, pos, kc, i, 3)
                before()

            pe.wait_ge(const_in, DMA * 3)
            pe.wait_ge(k_in, DMA * (len(PRODUCTS) + 1))
            for g in range(2):
                pe.wait_ge(q_in, (g + 1) * DMA * len(PRODUCTS))
                for t in range(NT):
                    for r in range(2):
                        max_scores(0, g, t, None, t, r)
            transpose_maxima(0)

            def body(qc, g, half, gg):
                n = item(qc, g)
                start = micro(qc, g)
                nxt = ahead(qc, half, gg)
                masks = n * NT
                if nxt:
                    pe.wait_ge(q_in, (n + 3) * (DMA * len(PRODUCTS)))
                    if half == 1:
                        pe.wait_ge(k_in, (qc + 2) * DMA * (len(PRODUCTS) + 1))
                pe.wait_ge(m_placed, n + 1)
                first = isinstance(n, int) and n == 0
                diagonal = qc == 0 or (qc == 1 and g == 0)
                for i in range(NT):
                    if i == 0:
                        def before():
                            if not first:
                                weigh(start - 1, NT - 1, diagonal, masks, False, True, None)
                    else:
                        def before(i=i):
                            weigh(start + (i - 1), i - 1, True, masks + i, i == 1, False, n)
                    step((qc, g), start + i, i, None, i, nxt, None, i, before)
                    if i == 1 and not (isinstance(n, int) and n + 1 == NCH * NG):
                        transpose_maxima(n + 1)
                extra = 1 if half == 1 and nxt else 0
                if extra:
                    for t in range(NT):
                        for r in range(2):
                            max_scores(*nxt, NT + t, 0, t, r)

                if qc:
                    for i in range(NT):
                        def before(i=i):
                            if i == 0:
                                weigh(start + (NT - 1), NT - 1, True, masks + NT, False, False, None)
                            else:
                                weigh(start + (NT + i - 1), i - 1, False, None, False, False, None)
                        step((qc, g), start + (NT + i), NT + i, 0, i, nxt, extra, NT + i + extra * NT, before)

                    def later(kc):
                        for i in range(NT):
                            pos = kc * NT + (NT + i)

                            def before(i=i):
                                weigh(start + (kc * NT + (NT + i - 1)), (i - 1) % NT, False, None, False, False,
                                      None)
                            step((qc, g), start + pos, pos, kc, i, nxt, kc + extra, pos + extra * NT, before)

                    if qc == 2:
                        later(1)
                    elif qc > 2:
                        with pe.Fori(1, qc) as kc:
                            later(kc)

            def project(c):
                pe.wait_ge(on_ready, (c + 1) * NG)
                reads = 2 * micro(min(c + 2, NCH), 0)
                pe.wait_ge(s1_read, reads)
                for t in range(NT):
                    for g in range(NG):
                        slot = c % 2 if g == 0 else g + 1
                        last = mm(s1[:, t, 0:C], on[:, slot * CH + t * P:slot * CH + (t + 1) * P],
                                  w_out[:, g, :], start=(g == 0), stop=(g == NG - 1))
                    last.then_inc(proj_ready, 1)
                pe.wait_ge(proj_added, (c + 1) * NT)

            items(pe, body, lambda qc: project(qc - 1) if qc else None)
            weigh(micro(NCH, 0) - 1, NT - 1, False, None, False, True, None)
            project(NCH - 1)

        @block.scalar
        def _(act):
            def exps(qc, g, pos, q0, i):
                mu = micro(qc, g, pos)
                for j in range(J):
                    act.wait_ge(s2_ready, mu * 4 + (j + 1))
                    if j == 0:
                        wait(act, av_done, mu - 1)
                    nc.scalar.activation(probs[:, i % 2, j, q0:CH], s2[:, j % 2, q0:CH], ACT.Exp,
                                         scale=SCALE).then_inc(exp_done, 1)

            def place_maxima(n, slot):
                act.wait_ge(mt_ready, n + 1)
                dst = q_st[SK:SM, bass.ds(slot * (J * CH), J * CH)].rearrange("p (j t) -> p j t", j=J)
                nc.scalar.activation(dst, mt_ps[SK:SM, 0:CH].unsqueeze(1).broadcast_to([MR, J, CH]),
                                     ACT.Copy).then_inc(m_placed, 1)

            place_maxima(0, 0)

            def body(qc, g, half, gg):
                n = item(qc, g)
                for i in range(NT):
                    exps(qc, g, i, i * P, i)
                    if i == 2 and not (isinstance(n, int) and n + 1 == NCH * NG):
                        place_maxima(n + 1, gg + 1 if half == 0 else gg * -3 + 3)

                def full(kc):
                    for i in range(NT):
                        exps(qc, g, kc * NT + (NT + i), 0, i)
                full_chunks(act, qc, full)

            items(act, body, lambda qc: None)

        @block.gpsimd
        def _(pool):
            nc.gpsimd.memset(v_ring[:, :, :, :], 0.0).then_inc(set_up, 1)
            pool.wait_ge(set_up, 1)
            nc.gpsimd.memset(v_ring[:, :, :, D:D + 1], 1.0).then_inc(set_up, 1)
            nc.gpsimd.memset(mparts[:, :, :], 0.0).then_inc(set_up, 1)
            pool.wait_ge(set_up, 3)

            def place_v(qc, g, gg, pos, at, i):
                mu = micro(qc, g, pos)
                wait_apart(pool, av_done, mu - 3, set_up, 3)
                nc.gpsimd.tensor_copy(v_ring[:, i, :, 0:D],
                                      v_buf[:, bass.ds(gg * (NCH * 256) + at, J * D)]
                                      .rearrange("p (j d) -> p j d", j=J)).then_inc(v_ready, 1)

            def body(qc, g, half, gg):
                n = item(qc, g)
                pool.wait_ge(v_in, (n + 1) * DMA)
                for i in range(NT):
                    place_v(qc, g, gg, i, qc * 256 + i * (J * D), i)
                    pool.wait_ge(exp_done, micro(qc, g, i) * 4 + 4)
                    sq = probs[:, i % 2, :, i * P:(i + 1) * P]
                    nc.gpsimd.affine_select(out=sq, in_=sq, compare_op=ALU.is_ge, fill=0.0, base=0,
                                            pattern=[[0, J], [1, P]], channel_multiplier=-1)\
                        .then_inc(mask_done, 1)
                    if i == 1 and not (isinstance(n, int) and n == 0):
                        normalise(n)

                def full(kc):
                    for i in range(NT):
                        place_v(qc, g, gg, kc * NT + (NT + i), kc * 256 + i * (J * D), i)
                full_chunks(pool, qc, full)

            def normalise(n):
                pool.wait_ge(l_ready, n)
                o = o_t[:, :].rearrange("p (b c) -> p b c", c=32)[:, :, 0:D]
                nc.gpsimd.tensor_tensor(o, o, l_rec[:, :].unsqueeze(2).broadcast_to([P, CH // 32, D]),
                                        ALU.mult).then_inc(scaled, 1)

            items(pool, body, lambda qc: None, peeled=True)
            normalise(NCH * NG)

        @block.vector
        def _(dve):
            v = nc.vector

            def reduce_pair(qc, g, pos, kc, t, r):
                pair = micro(qc, g, pos) * 2 + r
                dve.wait_ge(s1_ready, pair + 1)
                if kc is None:
                    n = P * (t + 1)
                    wait(dve, s1_read, pair)
                    for j in (2 * r, 2 * r + 1):
                        last = v.tensor_tensor_reduce(
                            out=masked[:, j % 2, 0:n], in0=s1[:, j, 0:n], in1=mask[:, CH - n:CH], scale=1.0,
                            scalar=NEG, op0=ALU.add, op1=ALU.max, accum_out=maxes[:, 0, t * J + j:t * J + j + 1])
                else:
                    slot = maxes[:, bass.ds(kc + 1, 1), t * J + 2 * r:t * J + 2 * r + 2].rearrange("p a b -> p (a b)")
                    last = v.tensor_reduce(out=slot, in_=s1[:, 2 * r:2 * r + 2, :], axis=AX.X, op=ALU.max)
                last.then_inc(s1_read, 1)

            def split_maxima(qc, g):
                n = item(qc, g)
                done = [0]

                def link(ins):
                    done[0] += 1
                    ins.then_inc(split_step, 1)
                    dve.wait_ge(split_step, n * SPLIT_STEPS + done[0])

                dve.wait_ge(s1_read, (micro(qc, g) + NT * (qc + 1)) * 2)
                wait(dve, m_ready, n)
                link(v.tensor_reduce(out=negmax[:, :], in_=maxes[:, 0:qc + 1, :].rearrange("p k c -> p c k"),
                                     axis=AX.X, op=ALU.max, negate=True))
                wait(dve, mt_ready, n)
                part = mparts[:, :, SK:SM].rearrange("p t (j r) -> p t j r", r=3)
                full = negmax[:, :].rearrange("p (t j) -> p t j", j=J)
                left = negrest[:, :].rearrange("p (t j) -> p t j", j=J)
                link(v.tensor_copy(part[:, :, :, 0], full))
                link(v.tensor_tensor(left, full, part[:, :, :, 0], ALU.subtract))
                link(v.tensor_copy(part[:, :, :, 1], left))
                v.tensor_tensor(part[:, :, :, 2], left, part[:, :, :, 1], ALU.subtract).then_inc(m_ready, 1)
                assert done[0] == SPLIT_STEPS

            def take_acc(n, start):
                dve.wait_ge(av_done, start)
                wait(dve, on_ready, n - 1)
                v.transpose(o_t[:, :], acc[:, :]).then_inc(acc_read, 1)

            def invert_sums(n):
                dve.wait_ge(acc_read, n)
                v.reciprocal(l_rec[:, :], o_t[:, :].rearrange("p (b c) -> p b c", c=32)[:, :, D]).then_inc(l_ready, 1)

            def put_back(n, slot, used):
                dve.wait_ge(scaled, n)
                wait(dve, proj_ready, used)
                v.transpose(on[:, bass.ds(slot * CH, CH)], o_t[:, :]).then_inc(on_ready, 1)

            dve.wait_ge(set_up, 3)
            dve.wait_ge(const_in, DMA * 3)
            for g in range(2):
                for t in range(NT):
                    for r in range(2):
                        reduce_pair(0, g, t, None, t, r)
                split_maxima(0, g)

            def body(qc, g, half, gg):
                n = item(qc, g)
                nxt = ahead(qc, half, gg)
                old = not (isinstance(n, int) and n == 0)
                for i in range(NT):
                    for r in range(2):
                        if nxt:
                            reduce_pair(*nxt, i, None, i, r)
                    if i == 0 and old:
                        take_acc(n, micro(qc, g))
                    if i == 1 and old:
                        invert_sums(n)
                    if i == 3 and old:
                        if half == 0:
                            put_back(n, gg * (qc % 2 - NG) + NG, (qc - 1) * NT)
                        else:
                            put_back(n, gg + 2, qc * NT)
                if nxt:
                    extra = 1 if half == 1 else 0
                    if extra:
                        for t in range(NT):
                            for r in range(2):
                                reduce_pair(*nxt, NT + t, 0, t, r)

                    def full(kc):
                        for i in range(NT):
                            for r in range(2):
                                reduce_pair(*nxt, kc * NT + (NT + i + extra * NT), kc + extra, i, r)
                    full_chunks(dve, qc, full)
                    split_maxima(*nxt)

            def add_projection(c):
                dve.wait_ge(rest_in, (c + 1) * DMA)
                for t in range(NT):
                    dve.wait_ge(proj_ready, c * NT + t + 1)
                    v.tensor_tensor(rest[:, t, :], s1[:, t, 0:C], rest[:, t, :], ALU.add).then_inc(proj_added, 1)

            items(dve, body, lambda qc: add_projection(qc - 1) if qc else None, peeled=True)
            n = NCH * NG
            take_acc(n, micro(NCH, 0))
            invert_sums(n)
            put_back(n, NG, (NCH - 1) * NT)
            add_projection(NCH - 1)


def build(nc, io, out):
    parts_d = nc.dram_tensor("qk_parts", (6 * C, T), BF16).ap()
    v_d = nc.dram_tensor("v_scratch", (NG * P, NCH * 256), F32).ap()
    rest_d = nc.dram_tensor("rest_scratch", (T, C), F32).ap()
    scratch = (parts_d, v_d, rest_d)
    layernorm_projections(nc, io, scratch)
    attention(nc, io, scratch, out)


def kernel(**inputs):
    import ml_dtypes
    import numpy as np
    import concourse.bacc as bacc
    from concourse.bass_utils import run_bass_kernel_spmd

    def halves(w):
        return w.reshape(E, 2, P, -1).transpose(0, 2, 1, 3).reshape(E * P, -1)

    a = {k.replace("L0_ffn_", "").replace("L0_attn_", ""): np.asarray(v) for k, v in inputs.items()}
    up = np.concatenate([a["up_W"].transpose(0, 2, 1), a["up_b"][:, :, None]], axis=2)
    w_out = np.zeros((NG, J, 32, C), np.float32)
    w_out[:, :, 0:D, :] = a["w_out"].reshape(NG, J, D, C)
    head_rows = np.repeat(np.eye(J, dtype=ml_dtypes.bfloat16), 3, axis=0)
    head_rows = np.repeat(np.tile(head_rows, (1, NG)), CH, axis=1)
    mask = np.zeros((P, CH), ml_dtypes.bfloat16)
    mask[:, CH - P:][np.triu_indices(P, 1)] = NEG
    arrays = {
        "x": a["x"].reshape(T, C),
        "w_qkv": a["w_qkv"],
        "w_out": w_out.reshape(NG * P, C),
        "base_W": a["base_W"].T,
        "base_b": a["base_b"].reshape(1, C),
        "disc_mu": a["disc_mu"].T,
        "disc_sigma": a["disc_sigma"].T,
        "down_W": halves(a["down_W"]),
        "down_b": a["down_b"].reshape(E * R, 1),
        "up_W": halves(up),
        "conv_W": halves(a["conv_W"].transpose(0, 2, 1)),
        "conv_b": a["conv_b"],
        "identity": np.eye(P, dtype=np.float32),
        "identity_b": np.eye(P, dtype=ml_dtypes.bfloat16),
        "mask": mask,
        "head_rows": head_rows,
    }
    arrays = {k: np.ascontiguousarray(v) for k, v in arrays.items()}
    nc = bacc.Bacc("TRN2", target_bir_lowering=False, num_devices=1)
    io = {k: nc.dram_tensor(f"in_{k}", v.shape, mybir.dt.from_np(v.dtype), kind="ExternalInput").ap()
          for k, v in arrays.items()}
    out = nc.dram_tensor("out_0", (T, C), F32, kind="ExternalOutput").ap()
    build(nc, io, out)
    r = run_bass_kernel_spmd(nc, [{f"in_{k}": v for k, v in arrays.items()}], core_ids=[0])
    return r.results[0]["out_0"].reshape(1, T, C)
```

```python
import concourse.bass as bass
from concourse import mybir
from contextlib import ExitStack

F32 = mybir.dt.float32
BF16 = mybir.dt.bfloat16
U32 = mybir.dt.uint32
ACT = mybir.ActivationFunctionType
ALU = mybir.AluOpType
AX = mybir.AxisListType

T = 4096
C = 256
HEADS = 16
D = C // HEADS
E = 8
R = 64
P = 128
CH = 512
NCH = T // CH
NT = CH // P
J = 4
NG = HEADS // J
EPS = 1e-5
NEG = -3.0e38
SCALE = 0.25

PRODUCTS = [(0, 0), (0, 1), (1, 0), (1, 1), (0, 2), (2, 0)]
SK = D * len(PRODUCTS)
MR = 3 * J
SM = SK + MR

DMA = 16
Q_COUNT = DMA * len(PRODUCTS)
K_COUNT = DMA * (len(PRODUCTS) + 1)


def micro(qc, g, pos=0):
    return 2 * NT * qc * (qc + 1) + g * (NT * (qc + 1)) + pos


def item(qc, g):
    return NG * qc + g


def wait(eng, sem, value):
    if not isinstance(value, int) or value > 0:
        eng.wait_ge(sem, value)


def wait_apart(eng, sem, value, true_sem, true_value):
    wait(eng, sem, value)
    eng.wait_ge(true_sem, true_value)


def layernorm_projections(nc, io, scratch, first_loads):
    parts_d, v_d, rest_d = scratch
    with ExitStack() as ctx:
        def sb(name, shape, dt=F32):
            return ctx.enter_context(nc.sbuf_tensor(name, shape, dt))

        def sem(name):
            return ctx.enter_context(nc.semaphore(name))

        x_sb = sb("x_sb", [P, NCH * NT, C])
        xn = sb("xn", [P, 2, NT, C])
        xs = sb("xs", [P, 2, 2, CH])
        xnT = sb("xnT", [P, 2, T])
        wqkv = sb("wqkv", [P, 2, 3 * C])
        wbase = sb("wbase", [P, 2, C])
        ident = sb("ident", [P, P])
        stats = sb("stats", [P, NT, 6])
        mv = sb("mv", [P, NT, 2])
        var = sb("var", [P, NT])
        std = sb("std", [P, NT])
        rs = sb("rs", [P, NT])
        tq = sb("tq", [P, NT])
        ts2 = sb("ts2", [P, NT])
        th = sb("th", [P, NT])
        rstd = sb("rstd", [P, NT])
        sum1 = sb("sum1", [P, 2, NCH])
        sum2 = sb("sum2", [P, 2, NCH])
        junk = sb("junk", [P, 2, CH], BF16)
        stage = sb("stage", [P, 4, 3, CH], BF16)
        rest1 = sb("rest1", [P, 2, CH])
        vst = sb("vst", [P, 2, NG, NT, J * D])
        muT = sb("muT", [P, 2, E])
        sgT = sb("sgT", [P, 2, E])
        sq = sb("sq", [P, 2, E])
        iv = sb("iv", [P, 2, E])
        miv = sb("miv", [P, 2, E])
        m2iv = sb("m2iv", [P, 2, E])
        mmiv = sb("mmiv", [P, 2, E])
        ones = sb("ones", [P, 1])
        m1 = sb("m1", [P, 2])
        m2 = sb("m2", [P, 2])
        m1s = sb("m1s", [P, 2])
        m2s = sb("m2s", [P, 2])
        nloss = sb("nloss", [1, E])
        best = sb("best", [1, 8])
        index = sb("index", [1, 8], U32)
        wdown = sb("wdown", [P, 2, R])
        bdown = sb("bdown", [R, 1])
        wup = sb("wup", [P, 2, R + 1])
        wconv = sb("wconv", [P, 2, C])
        brow = sb("brow", [R + 1, C])
        bbase = sb("bbase", [R + 1, C])
        wuc0 = sb("wuc0", [R + 1, C])
        wuc = sb("wuc", [R + 1, C])
        hT = sb("hT", [R + 1, 2, CH])

        tp = ctx.enter_context(nc.psum_tensor("tp", [P, 2, CH], F32))
        qk_ps = ctx.enter_context(nc.psum_tensor("qk_ps", [P, 2, CH], F32))
        vb_ps = ctx.enter_context(nc.psum_tensor("vb_ps", [P, 4, CH], F32))

        x_in = [sem(f"x_in{n}") for n in range(2)]
        w_in = sem("w_in")
        ln_step = sem("ln_step")
        var_ready = sem("var_ready")
        std_ready = sem("std_ready")
        xn_ready = sem("xn_ready")
        tp_ready = sem("tp_ready")
        tp_copied = sem("tp_copied")
        tp_squared = sem("tp_squared")
        qk_ready = sem("qk_ready")
        part1_ready = sem("part1_ready")
        rest_ready = sem("rest_ready")
        part2_ready = sem("part2_ready")
        part3_ready = sem("part3_ready")
        parts_out = [sem(f"parts_out{n}") for n in range(4)]
        v_psum = sem("v_psum")
        v_staged = sem("v_staged")
        v_out = [sem(f"v_out{n}") for n in range(2)]
        base_ready = sem("base_ready")
        base_added = sem("base_added")
        set_up = sem("set_up")
        xnT_ready = sem("xnT_ready")
        mean_ready = sem("mean_ready")
        loss_step = sem("loss_step")
        loss_ready = sem("loss_ready")
        index_ready = sem("index_ready")
        expert_in = sem("expert_in")
        wuc_psum = sem("wuc_psum")
        wuc_ready = sem("wuc_ready")
        h_psum = sem("h_psum")
        h_ready = sem("h_ready")
        ffn_ready = sem("ffn_ready")
        ffn_added = sem("ffn_added")
        rest_out = sem("rest_out")
        block = ctx.enter_context(nc.Block())

        def chunks(eng, body, peeled=False):
            if peeled:
                for c in range(NCH):
                    body(c, c % 2)
                return
            body(0, 0)
            body(1, 1)
            with eng.Fori(1, NCH // 2 - 1) as pair:
                body(pair * 2, 0)
                body(pair * 2 + 1, 1)
            body(NCH - 2, 0)
            body(NCH - 1, 1)

        def x_rows(c):
            return io["x"][c * CH:(c + 1) * CH, :].rearrange("(t p) n -> p t n", p=P)

        W_COUNT = 8

        @block.sync
        def _(sp):
            for c in range(NCH):
                wait(sp, x_in[c % 2], DMA * (c // 2))
                sp.dma_start(x_sb[:, c * NT:(c + 1) * NT, :], x_rows(c)).then_inc(x_in[c % 2], DMA)

            def store(c, par):
                for u in range(4):
                    sp.wait_ge(part3_ready, c * 4 + (u + 1))
                    sp.dma_start(
                        parts_d[(u // 2) * 3 * C:(u // 2 + 1) * 3 * C, bass.ds(c * CH, CH)]
                        .rearrange("(s n) t -> n s t", s=3)[(u % 2) * P:(u % 2 + 1) * P],
                        stage[:, u, :, :]).then_inc(parts_out[u], DMA)
                sp.wait_ge(v_staged, c * NT + NT)
                sp.dma_start(v_d.rearrange("(g p) n -> p g n", p=P)[:, :, bass.ds(c * 256, 256)],
                             vst[:, par, :, :, :].rearrange("p g t n -> p g (t n)")).then_inc(v_out[par], DMA)

            chunks(sp, store)
            sp.wait_ge(index_ready, 1)
            expert = sp.value_load(index[0:1, 0:1], min_val=0, max_val=E - 1)
            sp.dma_start(wdown[:, :, :].rearrange("p a b -> p (a b)"),
                         io["down_W"][bass.ds(expert * P, P), :]).then_inc(expert_in, DMA)
            sp.dma_start(bdown[:, :], io["down_b"][bass.ds(expert * R, R), :]).then_inc(expert_in, DMA)
            sp.dma_start(wup[:, :, :].rearrange("p a b -> p (a b)"),
                         io["up_W"][bass.ds(expert * P, P), :]).then_inc(expert_in, DMA)
            sp.dma_start(wconv[:, :, :].rearrange("p a b -> p (a b)"),
                         io["conv_W"][bass.ds(expert * P, P), :]).then_inc(expert_in, DMA)
            sp.dma_start(brow[R:R + 1, :], io["conv_b"][bass.ds(expert, 1), :]).then_inc(expert_in, DMA)

            def store_rest(c, par):
                sp.wait_ge(ffn_added, c * NT + NT)
                sp.dma_start(rest_d[bass.ds(c * CH, CH), :].rearrange("(t p) n -> p t n", p=P),
                             x_sb[:, bass.ds(c * NT, NT), :]).then_inc(rest_out, DMA)

            for u in range(4):
                sp.wait_ge(parts_out[u], DMA * NCH)
            for n in range(2):
                sp.wait_ge(v_out[n], DMA * NCH // 2)
            first_loads(sp)
            chunks(sp, store_rest)
            sp.wait_ge(rest_out, DMA * NCH)

        @block.scalar
        def _(act):
            act.dma_start(ident[:, :], io["identity"]).then_inc(w_in, DMA)
            act.dma_start(wqkv[:, :, :], io["w_qkv"].rearrange("(a p) n -> p a n", p=P)).then_inc(w_in, DMA)
            act.dma_start(wbase[:, :, :], io["base_W"].rearrange("(a p) n -> p a n", p=P)).then_inc(w_in, DMA)
            act.dma_start(muT[:, :, :], io["disc_mu"].rearrange("(a p) n -> p a n", p=P)).then_inc(w_in, DMA)
            act.dma_start(sgT[:, :, :], io["disc_sigma"].rearrange("(a p) n -> p a n", p=P)).then_inc(w_in, DMA)
            act.wait_ge(set_up, 1)
            act.dma_start(bbase[R:R + 1, :], io["base_b"]).then_inc(w_in, DMA)

            def root(c):
                act.wait_ge(var_ready, c + 1)
                nc.scalar.activation(std[:, :], var[:, :], ACT.Sqrt).then_inc(std_ready, 1)

            def take_transposed(c, par):
                for h in range(2):
                    act.wait_ge(tp_ready, c * 2 + (h + 1))
                    if not isinstance(c, int) or c >= 2:
                        act.wait_ge(base_ready, (c - 1) * NT)
                        act.wait_ge(xnT_ready, c - 1)
                    nc.scalar.activation(xs[:, par, h, :], tp[:, h, :], ACT.Copy,
                                         accum_out=sum1[:, h, bass.ds(c, 1)]).then_inc(tp_copied, 1)
                    wait(act, tp_squared, c * 2 + (h - 1))
                    nc.scalar.activation(junk[:, h, :], tp[:, h, :], ACT.Square,
                                         accum_out=sum2[:, h, bass.ds(c, 1)]).then_inc(tp_squared, 1)

            root(0)
            root(1)
            take_transposed(0, 0)

            def body(c, par):
                if not isinstance(c, int) or c + 2 < NCH:
                    root(c + 2)
                if not isinstance(c, int) or c + 1 < NCH:
                    take_transposed(c + 1, 1 - par)
                for u in range(4):
                    act.wait_ge(qk_ready, c * 4 + (u + 1))
                    wait(act, parts_out[u], c * DMA)
                    nc.scalar.activation(stage[:, u, 0, :], qk_ps[:, u % 2, :], ACT.Copy).then_inc(part1_ready, 1)
                for t in range(NT):
                    act.wait_ge(v_psum, c * NT + (t + 1))
                    if t == 0 and (not isinstance(c, int) or c >= 2):
                        act.wait_ge(v_out[par], (c - par) * (DMA // 2))
                    nc.scalar.activation(vst[:, par, :, t, :],
                                         vb_ps[:, t % 2, 0:C].rearrange("p (g n) -> p g n", g=NG),
                                         ACT.Copy).then_inc(v_staged, 1)

            chunks(act, body)

        @block.gpsimd
        def _(pool):
            def body(c, par):
                pool.wait_ge(tp_copied, c * 2 + 2)
                nc.gpsimd.tensor_copy(xnT[:, :, bass.ds(c * CH, CH)], xs[:, par, :, :]).then_inc(xnT_ready, 1)
                for u in range(4):
                    n = c * 4 + u
                    wait(pool, parts_out[u], c * DMA)
                    pool.wait_ge(part2_ready, n + 1)
                    nc.gpsimd.tensor_tensor(stage[:, u, 2, :], rest1[:, u % 2, :], stage[:, u, 1, :],
                                            ALU.subtract).then_inc(part3_ready, 1)

            chunks(pool, body, peeled=True)

        @block.vector
        def _(dve):
            v = nc.vector
            v.memset(brow[:, :], 0.0)
            v.memset(ones[:, :], 1.0)
            v.memset(hT[R:R + 1, :, :], 1.0)
            v.memset(bbase[:, :], 0.0).then_inc(set_up, 1)
            LN_STEPS = 7

            def layernorm(c, par):
                step = [0]

                def link(ins):
                    step[0] += 1
                    ins.then_inc(ln_step, 1)
                    dve.wait_ge(ln_step, c * LN_STEPS + step[0])

                dve.wait_ge(x_in[par], (c - par) * (DMA // 2) + DMA)
                wait(dve, xn_ready, c)
                for t in range(NT):
                    last = v.bn_stats(stats[:, t, :], x_sb[:, bass.ds(c * NT + t, 1), :]
                                      .rearrange("p a n -> p (a n)"))
                link(last)
                for t in range(NT):
                    last = v.bn_aggr(mv[:, t, :], stats[:, t, :])
                link(last)
                v.tensor_scalar(var[:, :], mv[:, :, 1], EPS, None, ALU.add).then_inc(var_ready, 1)
                dve.wait_ge(std_ready, c + 1)
                link(v.reciprocal(rs[:, :], std[:, :]))
                link(v.tensor_tensor(tq[:, :], var[:, :], rs[:, :], ALU.mult))
                link(v.tensor_tensor(ts2[:, :], tq[:, :], std[:, :], ALU.add))
                link(v.tensor_scalar(th[:, :], ts2[:, :], 0.5, None, ALU.mult))
                link(v.reciprocal(rstd[:, :], th[:, :]))
                assert step[0] == LN_STEPS
                if not isinstance(c, int) or c >= 2:
                    dve.wait_ge(tp_ready, (c - 1) * 2)
                for t in range(NT):
                    last = v.tensor_scalar(xn[:, par, t, :], x_sb[:, bass.ds(c * NT + t, 1), :]
                                           .rearrange("p a n -> p (a n)"),
                                           mv[:, t, 0:1], rstd[:, t:t + 1], ALU.subtract, ALU.mult)
                last.then_inc(xn_ready, 1)

            layernorm(0, 0)
            layernorm(1, 1)

            def body(c, par):
                if c + 2 < NCH:
                    layernorm(c + 2, par)
                for u in range(4):
                    n = c * 4 + u
                    dve.wait_ge(part1_ready, n + 1)
                    wait(dve, part3_ready, n - 1)
                    v.tensor_tensor(rest1[:, u % 2, :], qk_ps[:, u % 2, :], stage[:, u, 0, :],
                                    ALU.subtract).then_inc(rest_ready, 1)
                    wait(dve, parts_out[u], c * DMA)
                    dve.wait_ge(rest_ready, n + 1)
                    v.tensor_copy(stage[:, u, 1, :], rest1[:, u % 2, :]).then_inc(part2_ready, 1)
                for t in range(NT):
                    dve.wait_ge(base_ready, c * NT + (t + 1))
                    xt = x_sb[:, bass.ds(c * NT + t, 1), :].rearrange("p a n -> p (a n)")
                    v.tensor_tensor(xt, vb_ps[:, 2 + t % 2, 0:C], xt, ALU.add).then_inc(base_added, 1)

            done = [0]

            def link(ins):
                done[0] += 1
                ins.then_inc(loss_step, 1)
                dve.wait_ge(loss_step, done[0])

            dve.wait_ge(w_in, DMA * 6)
            link(v.tensor_tensor(sq[:, :, :], sgT[:, :, :], sgT[:, :, :], ALU.mult))
            link(v.reciprocal(iv[:, :, :], sq[:, :, :]))
            link(v.tensor_tensor(miv[:, :, :], muT[:, :, :], iv[:, :, :], ALU.mult))
            link(v.tensor_scalar(m2iv[:, :, :], miv[:, :, :], -2.0, None, ALU.mult))
            link(v.tensor_tensor(mmiv[:, :, :], miv[:, :, :], muT[:, :, :], ALU.mult))

            def means():
                dve.wait_ge(tp_squared, 2 * NCH)
                link(v.tensor_reduce(out=m1s[:, :], in_=sum1[:, :, :], axis=AX.X, op=ALU.add))
                link(v.tensor_reduce(out=m2s[:, :], in_=sum2[:, :, :], axis=AX.X, op=ALU.add))
                link(v.tensor_scalar(m1[:, :], m1s[:, :], 1.0 / T, None, ALU.mult))
                v.tensor_scalar(m2[:, :], m2s[:, :], 1.0 / T, None, ALU.mult).then_inc(mean_ready, 1)

            def choose():
                dve.wait_ge(loss_ready, 1)
                link(v.tensor_scalar(nloss[:, :], tp[0:1, 0, 0:E], -1.0 / C, None, ALU.mult))
                link(v.max(best[:, :], nloss[:, :]))
                v.max_index(index[:, :], best[:, :], nloss[:, :]).then_inc(index_ready, 1)

            for c in range(NCH):
                body(c, c % 2)
                if c == NCH - 2:
                    means()
                    choose()
            dve.wait_ge(wuc_psum, 1)
            link(v.tensor_tensor(wuc0[:, :], tp[0:R + 1, 1, 0:C], brow[:, :], ALU.add))
            v.tensor_tensor(wuc[:, :], wuc0[:, :], bbase[:, :], ALU.add).then_inc(wuc_ready, 1)

            def hidden(c, par):
                dve.wait_ge(h_psum, c + 1)
                if c >= 2:
                    dve.wait_ge(ffn_ready, (c - 1) * NT)
                v.tensor_scalar(hT[0:R, par, :], qk_ps[0:R, par, :], bdown[:, 0:1], 0.0,
                                ALU.add, ALU.max).then_inc(h_ready, 1)

            def ffn(c, par):
                if c + 1 < NCH:
                    hidden(c + 1, 1 - par)
                for t in range(NT):
                    dve.wait_ge(ffn_ready, c * NT + (t + 1))
                    xt = x_sb[:, bass.ds(c * NT + t, 1), :].rearrange("p a n -> p (a n)")
                    v.tensor_tensor(xt, vb_ps[:, t, 0:C], xt, ALU.add).then_inc(ffn_added, 1)

            dve.wait_ge(base_added, NT * NCH)
            hidden(0, 0)
            chunks(dve, ffn, peeled=True)

        @block.tensor
        def _(pe):
            pe.wait_ge(w_in, DMA * 6)

            def transpose(c, par):
                pe.wait_ge(xn_ready, c + 1)
                for h in range(2):
                    wait(pe, tp_squared, c * 2 - 1 + h)
                    for t in range(NT):
                        last = nc.tensor.transpose(tp[:, h, t * P:(t + 1) * P],
                                                   xn[:, par, t, h * P:(h + 1) * P], ident[:, :])
                    last.then_inc(tp_ready, 1)

            def choose():
                pe.wait_ge(mean_ready, 1)
                terms = [(m2[:, h:h + 1], iv[:, h, :]) for h in range(2)]
                terms += [(m1[:, h:h + 1], m2iv[:, h, :]) for h in range(2)]
                terms += [(ones[:, :], mmiv[:, h, :]) for h in range(2)]
                for n, (a, b) in enumerate(terms):
                    last = nc.tensor.matmul(tp[0:1, 0, 0:E], a, b, start=(n == 0), stop=(n == len(terms) - 1))
                last.then_inc(loss_ready, 1)

            transpose(0, 0)

            def body(c, par):
                if not isinstance(c, int) or c + 1 < NCH:
                    transpose(c + 1, 1 - par)
                else:
                    choose()
                pe.wait_ge(tp_copied, c * 2 + 2)
                for u in range(4):
                    n = c * 4 + u
                    wait(pe, rest_ready, n - 1)
                    for h in range(2):
                        last = nc.tensor.matmul(qk_ps[:, u % 2, :], wqkv[:, h, u * P:(u + 1) * P],
                                                xs[:, par, h, :], start=(h == 0), stop=(h == 1))
                    last.then_inc(qk_ready, 1)
                for t in range(NT):
                    wait(pe, v_staged, c * NT + (t - 1))
                    for h in range(2):
                        last = nc.tensor.matmul(vb_ps[:, t % 2, 0:C], xs[:, par, h, t * P:(t + 1) * P],
                                                wqkv[:, h, 2 * C:3 * C], start=(h == 0), stop=(h == 1))
                    last.then_inc(v_psum, 1)
                    wait(pe, base_added, c * NT + (t - 1))
                    for h in range(2):
                        last = nc.tensor.matmul(vb_ps[:, 2 + t % 2, 0:C], xs[:, par, h, t * P:(t + 1) * P],
                                                wbase[:, h, :], start=(h == 0), stop=(h == 1))
                    last.then_inc(base_ready, 1)

            chunks(pe, body)
            pe.wait_ge(expert_in, DMA * 5)
            for h in range(2):
                last = nc.tensor.matmul(tp[0:R + 1, 1, 0:C], wup[:, h, :], wconv[:, h, :],
                                        start=(h == 0), stop=(h == 1))
            last.then_inc(wuc_psum, 1)
            pe.wait_ge(xnT_ready, NCH)
            pe.wait_ge(v_staged, NCH * NT)
            pe.wait_ge(base_added, NCH * NT)
            pe.wait_ge(rest_ready, NCH * 4)
            pe.wait_ge(wuc_ready, 1)

            def hidden(c, par):
                wait(pe, h_ready, c - 1)
                for h in range(2):
                    last = nc.tensor.matmul(qk_ps[0:R, par, :], wdown[:, h, :],
                                            xnT[:, h, bass.ds(c * CH, CH)], start=(h == 0), stop=(h == 1))
                last.then_inc(h_psum, 1)

            def ffn(c, par):
                if not isinstance(c, int) or c + 1 < NCH:
                    hidden(c + 1, 1 - par)
                pe.wait_ge(h_ready, c + 1)
                for t in range(NT):
                    wait(pe, ffn_added, c * NT + (t - 3))
                    nc.tensor.matmul(vb_ps[:, t, 0:C], hT[:, par, t * P:(t + 1) * P], wuc[:, :],
                                     start=True, stop=True).then_inc(ffn_ready, 1)

            hidden(0, 0)
            chunks(pe, ffn)


class FirstLoads:

    def __init__(self, nc, ctx, io, scratch):
        def sb(name, shape, dt=F32):
            return ctx.enter_context(nc.sbuf_tensor(name, shape, dt))

        self.io, (self.parts_d, self.v_d, _) = io, scratch
        self.k_0 = sb("k_0", [P, HEADS * CH], BF16)
        self.q_st = sb("q_st", [P, NG * J * CH], BF16)
        self.v_buf = sb("v_buf", [P, 2 * NCH * NT * J * D])
        self.k_in, self.q_in, self.v_in = (ctx.enter_context(nc.semaphore(n)) for n in ("k_in", "q_in", "v_in"))

    def load_k(self, sp, c, into):
        wait(sp, self.k_in, c * K_COUNT)
        kv = into.rearrange("p (h t) -> p h t", h=HEADS)
        for n, (_, part) in enumerate(PRODUCTS):
            src = self.parts_d[(3 + part) * C:(4 + part) * C, c * CH:(c + 1) * CH]
            sp.dma_start(kv[n * D:(n + 1) * D], src.rearrange("(h d) t -> d h t", d=D)).then_inc(self.k_in, DMA)
        sp.dma_start(kv[SK:SM], self.io["head_rows"].rearrange("r (h t) -> r h t", h=HEADS))\
          .then_inc(self.k_in, DMA)

    def load_q(self, sp, n, qc, g):
        wait(sp, self.q_in, n * Q_COUNT)
        for r, (part, _) in enumerate(PRODUCTS):
            src = self.parts_d[part * C + g * J * D:part * C + (g + 1) * J * D, qc * CH:(qc + 1) * CH]
            sp.dma_start(self.q_st[r * D:(r + 1) * D, g * J * CH:(g + 1) * J * CH]
                         .rearrange("p (j t) -> p j t", j=J),
                         src.rearrange("(j d) t -> d j t", d=D)).then_inc(self.q_in, DMA)

    def load_v(self, sp, n, g, count):
        wait(sp, self.v_in, n * DMA)
        sp.dma_start(self.v_buf[:, (n % 2) * NCH * 256:(n % 2) * NCH * 256 + count * 256],
                     self.v_d[g * P:(g + 1) * P, 0:count * 256]).then_inc(self.v_in, DMA)

    def start(self, sp):
        self.load_k(sp, 0, self.k_0[:, :])
        for g in range(3):
            self.load_q(sp, g, 0, g)
        self.load_v(sp, 0, 0, 1)


def attention(nc, io, scratch, out, loads):
    parts_d, v_d, rest_d = scratch
    with ExitStack() as ctx:
        def sb(name, shape, dt=F32):
            return ctx.enter_context(nc.sbuf_tensor(name, shape, dt))

        def sem(name):
            return ctx.enter_context(nc.semaphore(name))

        q_st, v_buf, k_0 = loads.q_st, loads.v_buf, loads.k_0
        k_in, q_in, v_in = loads.k_in, loads.q_in, loads.v_in
        k_st = sb("k_st", [P, (NCH - 1) * HEADS * CH], BF16)
        v_ring = sb("v_ring", [P, NT, J, 32])
        probs = sb("probs", [P, 2, J, CH])
        on = sb("on", [P, (NG + 2) * CH])
        o_t = sb("o_t", [P, CH])
        l_rec = sb("l_rec", [P, CH // 32])
        rest = sb("rest", [P, NT, C])
        w_out = sb("w_out", [P, NG, C])
        ident = sb("ident_b", [P, P], BF16)
        mask = sb("mask", [P, CH], BF16)
        masked = sb("masked", [P, 2, CH], BF16)
        maxes = sb("maxes", [P, NCH + 1, NT * J])
        negmax = sb("negmax", [P, NT * J])
        negrest = sb("negrest", [P, NT * J])
        mparts = sb("mparts", [P, NT, P], BF16)

        s1 = ctx.enter_context(nc.psum_tensor("s1", [P, 4, CH], F32))
        s2 = ctx.enter_context(nc.psum_tensor("s2", [P, 2, CH], F32))
        acc = ctx.enter_context(nc.psum_tensor("acc", [P, CH], F32))
        mt_ps = ctx.enter_context(nc.psum_tensor("mt_ps", [P, 2 * CH], BF16))

        proj_ps = mt_ps[:, 0:2 * C].bitcast(F32)

        const_in = sem("const_in")
        set_up = sem("set_up2")
        rest_in = sem("rest_in")
        s1_ready = sem("s1_ready")
        s1_read = sem("s1_read")
        split_step = sem("split_step")
        m_ready = sem("m_ready")
        mt_ready = sem("mt_ready")
        m_placed = sem("m_placed")
        s2_ready = sem("s2_ready")
        exp_done = sem("exp_done")
        mask_done = sem("mask_done")
        v_ready = sem("v_ready")
        av_done = sem("av_done")
        acc_read = sem("acc_read")
        l_ready = sem("l_ready")
        scaled = sem("scaled")
        on_ready = sem("on_ready")
        proj_ready = sem("proj_ready")
        proj_added = sem("proj_added")
        out_done = sem("out_done")
        block = ctx.enter_context(nc.Block())

        SPLIT_STEPS = 4

        def k_at(rows, g, j, kc, at, n):
            if isinstance(kc, int) and kc == 0:
                return k_0[0:rows, bass.ds((g * J + j) * CH + at, n)]
            return k_st[0:rows, bass.ds((kc - 1) * (HEADS * CH) + ((g * J + j) * CH + at), n)]

        def items(eng, body, peeled=False):
            for qc in range(NCH):
                for half in range(2):
                    if peeled or half == 1 or qc in (0, 1, NCH - 1):
                        for gg in range(2):
                            body(qc, 2 * half + gg, half, gg)
                    else:
                        with eng.Fori(0, 2) as gg:
                            body(qc, gg, half, gg)

        def turns(eng, first, count, body):
            if count - first == 1:
                body(first)
            elif count > first:
                with eng.Fori(first, count) as k:
                    body(k)

        def ahead(qc, half, gg):
            if half == 0:
                return qc, gg + 2
            return (qc + 1, gg) if qc + 1 < NCH else None

        def on_slot(qc, g):
            return 2 * g + qc % 2 if g < 2 else g + 2

        def tail(qc, g):
            return isinstance(g, int) and qc == NCH - 1 and g >= 2

        def s2_bank(qc, g, j):
            return s1[:, j, :] if tail(qc, g) else s2[:, j % 2, :]

        @block.sync
        def _(sp):
            sp.dma_start(ident[:, :], io["identity_b"]).then_inc(const_in, DMA)
            sp.dma_start(mask[:, :], io["mask"]).then_inc(const_in, DMA)
            sp.dma_start(w_out[:, :, :], io["w_out"].rearrange("(g p) n -> p g n", p=P)).then_inc(const_in, DMA)

            loads.load_k(sp, 1, k_st[:, 0:HEADS * CH])

            def body(qc, g, half, gg):
                n = item(qc, g)
                if g == 0 and qc + 2 < NCH:
                    loads.load_k(sp, qc + 2, k_st[:, (qc + 1) * HEADS * CH:(qc + 2) * HEADS * CH])
                if n + 3 < NCH * NG:
                    wait(sp, s2_ready, micro(qc, g) * 4)
                    loads.load_q(sp, n + 3, *divmod(n + 3, NG))
                if n + 1 < NCH * NG:
                    wait(sp, v_ready, micro(qc, g))
                    loads.load_v(sp, n + 1, (n + 1) % NG, (n + 1) // NG + 1)
                if g == 1 and qc > 0:
                    load_rest(qc - 1)
                if g == 2 and qc > 0:
                    store(qc - 1)

            def load_rest(c):
                wait(sp, out_done, c * NT * DMA)
                sp.dma_start(rest[:, :, :], rest_d[c * CH:(c + 1) * CH, :]
                             .rearrange("(t p) n -> p t n", p=P)).then_inc(rest_in, DMA)

            def store(c):
                for t in range(NT):
                    sp.wait_ge(proj_added, c * NT + t + 1)
                    sp.dma_start(out[c * CH + t * P:c * CH + (t + 1) * P, :],
                                 rest[:, t, :]).then_inc(out_done, DMA)

            items(sp, body, peeled=True)
            load_rest(NCH - 1)
            store(NCH - 1)
            sp.wait_ge(out_done, NCH * NT * DMA)

        @block.tensor
        def _(pe):
            mm = nc.tensor.matmul

            def max_scores(qc, g, pos, kc, t, r):
                n = P * (t + 1) if kc is None else CH
                wait(pe, s1_read, micro(qc, g, pos) * 2 + (r - 1))
                for j in (2 * r, 2 * r + 1):
                    last = mm(s1[:, j, 0:n], q_st[0:SK, bass.ds(g * (J * CH) + (j * CH + t * P), P)],
                              k_at(SK, g, j, qc if kc is None else kc, 0, n), start=True, stop=True)
                last.then_inc(s1_ready, 1)

            def scores(qc, g, pos, kc, i, j):
                q0 = i * P if kc is None else 0
                if tail(qc, g):
                    wait(pe, exp_done, micro(qc, g, pos) * 4 + (j - 3))
                else:
                    wait(pe, exp_done, micro(qc, g, pos) * 4 + (j - 1))
                mm(s2_bank(qc, g, j)[:, q0:CH], k_at(SM, g, j, qc if kc is None else kc, i * P, P),
                   q_st[0:SM, bass.ds(g * (J * CH) + (j * CH + q0), CH - q0)],
                   start=True, stop=True).then_inc(s2_ready, 1)

            def weigh(mu, i, diagonal, masks, first, final, taken):
                q0 = i * P if diagonal else 0
                if diagonal:
                    pe.wait_ge(mask_done, masks)
                else:
                    pe.wait_ge(exp_done, mu * 4 + 4)
                pe.wait_ge(v_ready, mu + 1)
                if first:
                    wait(pe, acc_read, taken)
                for j in range(J):
                    last = mm(acc[32 * j:32 * j + 32, q0:CH], v_ring[:, i, j, :], probs[:, i % 2, j, q0:CH],
                              start=first, stop=final, tile_position=(0, 32 * j))
                last.then_inc(av_done, 1)

            def transpose_maxima(n, projected):
                pe.wait_ge(m_ready, n + 1)
                wait(pe, m_placed, n)
                wait(pe, proj_added, projected * NT)
                for t in range(NT):
                    last = nc.tensor.transpose(mt_ps[:, t * P:(t + 1) * P], mparts[:, t, :], ident[:, :])
                last.then_inc(mt_ready, 1)

            def step(qc, g, pos, kc, i, ahead_step, late):
                for j in range(J):
                    scores(qc, g, pos, kc, i, j)
                    if j == 1:
                        ahead_step()
                late()

            def project(c, t):
                if t == 0:
                    pe.wait_ge(on_ready, (c + 1) * NG)
                    pe.wait_ge(m_placed, min((c + 1) * NG + 4, NCH * NG))
                wait(pe, proj_added, c * NT + t)
                for g in range(NG):
                    at = on_slot(c, g) * CH + t * P
                    last = mm(proj_ps, on[:, at:at + P],
                              w_out[:, g, :], start=(g == 0), stop=(g == NG - 1))
                last.then_inc(proj_ready, 1)

            pe.wait_ge(const_in, DMA * 3)
            pe.wait_ge(k_in, K_COUNT)
            for g in range(2):
                pe.wait_ge(q_in, (g + 1) * Q_COUNT)
                for t in range(NT):
                    for r in range(2):
                        max_scores(0, g, t, None, t, r)
            transpose_maxima(0, 0)

            def body(qc, g, half, gg):
                n = item(qc, g)
                start = micro(qc, g)
                nxt = ahead(qc, half, gg)
                extra = 1 if half == 1 else 0
                masks = n * NT
                final = isinstance(n, int) and n + 1 == NCH * NG
                if nxt:
                    pe.wait_ge(q_in, (n + 3) * Q_COUNT)
                    if half == 1:
                        pe.wait_ge(k_in, (qc + 2) * K_COUNT)
                pe.wait_ge(m_placed, n + 1)
                if tail(qc, g):
                    pe.wait_ge(s1_read, micro(NCH, 0) * 2)

                def max_step(pos, kc, t):
                    if nxt:
                        for r in range(2):
                            max_scores(*nxt, pos, kc, t, r)

                def no_step():
                    pass

                for i in range(NT):
                    def ahead_step():
                        max_step(i, 0 if nxt and nxt[0] else None, i)

                    def late():
                        if i:
                            weigh(start + (i - 1), i - 1, True, masks + i, i == 1, False, n)
                        elif not (isinstance(n, int) and n == 0):
                            weigh(start - 1, NT - 1, qc == 0 or (qc == 1 and isinstance(g, int) and g == 0),
                                  masks, False, True, None)
                    step(qc, g, i, None, i, ahead_step, late)
                    if i == 1 and not final:
                        transpose_maxima(n + 1, max(0, qc - (half == 0 or gg == 0)))
                if tail(qc, g) and gg == 0:
                    for t in range(NT):
                        project(qc - 1, t)
                for t in range(NT):
                    if nxt and extra:
                        max_step(NT + t, 1 if qc else None, t)
                        if gg == 0 and qc:
                            project(qc - 1, t)

                def full(k, late_diagonal):
                    pos = k * NT
                    last = isinstance(k, int) and k == qc
                    for i in range(NT):
                        def ahead_step():
                            max_step(pos + (i + extra * NT), None if last else k + extra, i)

                        def late():
                            if i == 0 and late_diagonal:
                                weigh(start + (NT - 1), NT - 1, True, masks + NT, False, False, None)
                            else:
                                weigh(start + (pos + (i - 1)), (i - 1) % NT, False, None, False, False, None)
                        step(qc, g, pos + i, k - 1, i, ahead_step, late)

                if qc > 1:
                    full(1, True)
                turns(pe, 2, qc, lambda k: full(k, False))
                if qc:
                    full(qc, qc == 1)

            items(pe, body, peeled=True)
            weigh(micro(NCH, 0) - 1, NT - 1, False, None, False, True, None)
            for t in range(NT):
                project(NCH - 1, t)

        @block.scalar
        def _(act):
            def exps(qc, g, pos, q0, i):
                mu = micro(qc, g, pos)
                for j in range(J):
                    act.wait_ge(s2_ready, mu * 4 + (j + 1))
                    if j == 0:
                        wait(act, av_done, mu - 1)
                    nc.scalar.activation(probs[:, i % 2, j, q0:CH], s2_bank(qc, g, j)[:, q0:CH], ACT.Exp,
                                         scale=SCALE).then_inc(exp_done, 1)

            def place_maxima(n, slot):
                act.wait_ge(mt_ready, n + 1)
                dst = q_st[SK:SM, bass.ds(slot * (J * CH), J * CH)].rearrange("p (j t) -> p j t", j=J)
                nc.scalar.activation(dst, mt_ps[SK:SM, 0:CH].unsqueeze(1).broadcast_to([MR, J, CH]),
                                     ACT.Copy).then_inc(m_placed, 1)

            place_maxima(0, 0)

            def body(qc, g, half, gg):
                n = item(qc, g)
                for i in range(NT):
                    exps(qc, g, i, i * P, i)
                    if i == 2 and not (isinstance(n, int) and n + 1 == NCH * NG):
                        place_maxima(n + 1, gg + 1 if half == 0 else gg * -3 + 3)

                def full(kc):
                    for i in range(NT):
                        exps(qc, g, kc * NT + (NT + i), 0, i)
                turns(act, 0, qc, full)

            items(act, body)

        @block.gpsimd
        def _(pool):
            nc.gpsimd.memset(v_ring[:, :, :, :], 0.0).then_inc(set_up, 1)
            pool.wait_ge(set_up, 1)
            nc.gpsimd.memset(v_ring[:, :, :, D:D + 1], 1.0).then_inc(set_up, 1)
            nc.gpsimd.memset(mparts[:, :, :], 0.0).then_inc(set_up, 1)
            pool.wait_ge(set_up, 3)

            def place_v(qc, g, gg, pos, at, i):
                mu = micro(qc, g, pos)
                wait_apart(pool, av_done, mu - 3, set_up, 3)
                nc.gpsimd.tensor_copy(v_ring[:, i, :, 0:D],
                                      v_buf[:, bass.ds(gg * (NCH * 256) + at, J * D)]
                                      .rearrange("p (j d) -> p j d", j=J)).then_inc(v_ready, 1)

            def body(qc, g, half, gg):
                n = item(qc, g)
                pool.wait_ge(v_in, (n + 1) * DMA)
                for i in range(NT):
                    place_v(qc, g, gg, i, qc * 256 + i * (J * D), i)
                    pool.wait_ge(exp_done, micro(qc, g, i) * 4 + 4)
                    sq = probs[:, i % 2, :, i * P:(i + 1) * P]
                    nc.gpsimd.affine_select(out=sq, in_=sq, compare_op=ALU.is_ge, fill=0.0, base=0,
                                            pattern=[[0, J], [1, P]], channel_multiplier=-1)\
                        .then_inc(mask_done, 1)
                    if i == 2 and n:
                        normalise(n)

                def full(kc):
                    for i in range(NT):
                        place_v(qc, g, gg, kc * NT + (NT + i), kc * 256 + i * (J * D), i)
                turns(pool, 0, qc, full)

            def normalise(n):
                pool.wait_ge(l_ready, n)
                o = o_t[:, :].rearrange("p (b c) -> p b c", c=32)[:, :, 0:D]
                nc.gpsimd.tensor_tensor(o, o, l_rec[:, :].unsqueeze(2).broadcast_to([P, CH // 32, D]),
                                        ALU.mult).then_inc(scaled, 1)

            items(pool, body, peeled=True)
            normalise(NCH * NG)

        @block.vector
        def _(dve):
            v = nc.vector

            def reduce_pair(qc, g, pos, kc, t, r):
                pair = micro(qc, g, pos) * 2 + r
                dve.wait_ge(s1_ready, pair + 1)
                if kc is None:
                    n = P * (t + 1)
                    wait(dve, s1_read, pair)
                    for j in (2 * r, 2 * r + 1):
                        last = v.tensor_tensor_reduce(
                            out=masked[:, j % 2, 0:n], in0=s1[:, j, 0:n], in1=mask[:, CH - n:CH], scale=1.0,
                            scalar=NEG, op0=ALU.add, op1=ALU.max, accum_out=maxes[:, 0, t * J + j:t * J + j + 1])
                else:
                    slot = maxes[:, bass.ds(kc + 1, 1), t * J + 2 * r:t * J + 2 * r + 2].rearrange("p a b -> p (a b)")
                    last = v.tensor_reduce(out=slot, in_=s1[:, 2 * r:2 * r + 2, :], axis=AX.X, op=ALU.max)
                last.then_inc(s1_read, 1)

            def split_maxima(qc, g):
                n = item(qc, g)
                done = [0]

                def link(ins):
                    done[0] += 1
                    ins.then_inc(split_step, 1)
                    dve.wait_ge(split_step, n * SPLIT_STEPS + done[0])

                dve.wait_ge(s1_read, (micro(qc, g) + NT * (qc + 1)) * 2)
                wait(dve, m_ready, n)
                link(v.tensor_reduce(out=negmax[:, :], in_=maxes[:, 0:qc + 1, :].rearrange("p k c -> p c k"),
                                     axis=AX.X, op=ALU.max, negate=True))
                wait(dve, mt_ready, n)
                part = mparts[:, :, SK:SM].rearrange("p t (j r) -> p t j r", r=3)
                full = negmax[:, :].rearrange("p (t j) -> p t j", j=J)
                left = negrest[:, :].rearrange("p (t j) -> p t j", j=J)
                link(v.tensor_copy(part[:, :, :, 0], full))
                link(v.tensor_tensor(left, full, part[:, :, :, 0], ALU.subtract))
                link(v.tensor_copy(part[:, :, :, 1], left))
                v.tensor_tensor(part[:, :, :, 2], left, part[:, :, :, 1], ALU.subtract).then_inc(m_ready, 1)
                assert done[0] == SPLIT_STEPS

            def take_acc(n, start):
                dve.wait_ge(av_done, start)
                wait(dve, on_ready, n - 1)
                v.transpose(o_t[:, :], acc[:, :]).then_inc(acc_read, 1)

            def invert_sums(n):
                dve.wait_ge(acc_read, n)
                v.reciprocal(l_rec[:, :], o_t[:, :].rearrange("p (b c) -> p b c", c=32)[:, :, D]).then_inc(l_ready, 1)

            def put_back(n):
                qc, g = divmod(n - 1, NG)
                slot = on_slot(qc, g)
                dve.wait_ge(scaled, n)
                wait(dve, proj_ready, (qc - 1 if g < 2 else qc) * NT)
                v.transpose(on[:, slot * CH:(slot + 1) * CH], o_t[:, :]).then_inc(on_ready, 1)

            dve.wait_ge(set_up, 3)
            dve.wait_ge(const_in, DMA * 3)
            for g in range(2):
                for t in range(NT):
                    for r in range(2):
                        reduce_pair(0, g, t, None, t, r)
                split_maxima(0, g)

            def body(qc, g, half, gg):
                n = item(qc, g)
                nxt = ahead(qc, half, gg)
                old = not (isinstance(n, int) and n == 0)
                extra = 1 if half == 1 else 0

                def max_step(pos, kc, t):
                    if nxt:
                        for r in range(2):
                            reduce_pair(*nxt, pos, kc, t, r)

                for i in range(NT):
                    max_step(i, 0 if nxt and nxt[0] else None, i)
                    if n:
                        if i == 0:
                            take_acc(n, micro(qc, g))
                        if i == 1:
                            invert_sums(n)
                        if i == 3:
                            put_back(n)
                if tail(qc, g) and gg == 0:
                    for t in range(NT):
                        add_projection(qc - 1, t)
                for t in range(NT):
                    if nxt and extra:
                        max_step(NT + t, 1 if qc else None, t)
                        if gg == 0 and qc:
                            add_projection(qc - 1, t)
                if nxt:
                    def full(k):
                        last = isinstance(k, int) and k == qc
                        for i in range(NT):
                            max_step(k * NT + (i + extra * NT), None if last else k + extra, i)
                    turns(dve, 1, qc, full)
                    if qc:
                        full(qc)
                    split_maxima(*nxt)

            def add_projection(c, t):
                if t == 0:
                    dve.wait_ge(rest_in, (c + 1) * DMA)
                dve.wait_ge(proj_ready, c * NT + t + 1)
                v.tensor_tensor(rest[:, t, :], proj_ps, rest[:, t, :], ALU.add).then_inc(proj_added, 1)

            items(dve, body, peeled=True)
            n = NCH * NG
            take_acc(n, micro(NCH, 0))
            invert_sums(n)
            put_back(n)
            for t in range(NT):
                add_projection(NCH - 1, t)


def build(nc, io, out):
    parts_d = nc.dram_tensor("qk_parts", (6 * C, T), BF16).ap()
    v_d = nc.dram_tensor("v_scratch", (NG * P, NCH * 256), F32).ap()
    rest_d = nc.dram_tensor("rest_scratch", (T, C), F32).ap()
    scratch = (parts_d, v_d, rest_d)
    with ExitStack() as ctx:
        loads = FirstLoads(nc, ctx, io, scratch)
        layernorm_projections(nc, io, scratch, loads.start)
        attention(nc, io, scratch, out, loads)


def kernel(**inputs):
    import ml_dtypes
    import numpy as np
    import concourse.bacc as bacc
    from concourse.bass_utils import run_bass_kernel_spmd

    def halves(w):
        return w.reshape(E, 2, P, -1).transpose(0, 2, 1, 3).reshape(E * P, -1)

    a = {k.replace("L0_ffn_", "").replace("L0_attn_", ""): np.asarray(v) for k, v in inputs.items()}
    up = np.concatenate([a["up_W"].transpose(0, 2, 1), a["up_b"][:, :, None]], axis=2)
    w_out = np.zeros((NG, J, 32, C), np.float32)
    w_out[:, :, 0:D, :] = a["w_out"].reshape(NG, J, D, C)
    head_rows = np.repeat(np.eye(J, dtype=ml_dtypes.bfloat16), 3, axis=0)
    head_rows = np.repeat(np.tile(head_rows, (1, NG)), CH, axis=1)
    mask = np.zeros((P, CH), ml_dtypes.bfloat16)
    mask[:, CH - P:][np.triu_indices(P, 1)] = NEG
    arrays = {
        "x": a["x"].reshape(T, C),
        "w_qkv": a["w_qkv"],
        "w_out": w_out.reshape(NG * P, C),
        "base_W": a["base_W"].T,
        "base_b": a["base_b"].reshape(1, C),
        "disc_mu": a["disc_mu"].T,
        "disc_sigma": a["disc_sigma"].T,
        "down_W": halves(a["down_W"]),
        "down_b": a["down_b"].reshape(E * R, 1),
        "up_W": halves(up),
        "conv_W": halves(a["conv_W"].transpose(0, 2, 1)),
        "conv_b": a["conv_b"],
        "identity": np.eye(P, dtype=np.float32),
        "identity_b": np.eye(P, dtype=ml_dtypes.bfloat16),
        "mask": mask,
        "head_rows": head_rows,
    }
    arrays = {k: np.ascontiguousarray(v) for k, v in arrays.items()}
    nc = bacc.Bacc("TRN2", target_bir_lowering=False, num_devices=1)
    io = {k: nc.dram_tensor(f"in_{k}", v.shape, mybir.dt.from_np(v.dtype), kind="ExternalInput").ap()
          for k, v in arrays.items()}
    out = nc.dram_tensor("out_0", (T, C), F32, kind="ExternalOutput").ap()
    build(nc, io, out)
    r = run_bass_kernel_spmd(nc, [{f"in_{k}": v for k, v in arrays.items()}], core_ids=[0])
    return r.results[0]["out_0"].reshape(1, T, C)
```

```python
import concourse.bass as bass
from concourse import mybir
from contextlib import ExitStack

F32 = mybir.dt.float32
BF16 = mybir.dt.bfloat16
U32 = mybir.dt.uint32
ACT = mybir.ActivationFunctionType
ALU = mybir.AluOpType
AX = mybir.AxisListType

T = 4096
C = 256
HEADS = 16
D = C // HEADS
E = 8
R = 64
P = 128
CH = 512
NCH = T // CH
NT = CH // P
J = 4
NG = HEADS // J
NP = NG // 2
EPS = 1e-5
NEG = -3.0e38
SCALE = 0.25

PRODUCTS = [(0, 0), (0, 1), (1, 0), (1, 1), (0, 2), (2, 0)]
SK = D * len(PRODUCTS)
MR = 3 * J
SM = SK + MR

DMA = 16
Q_COUNT = DMA * len(PRODUCTS)
K_COUNT = DMA * (len(PRODUCTS) + 1)


def micro(qc, g, pos=0):
    return 2 * NT * qc * (qc + 1) + g * (NT * (qc + 1)) + pos


def item(qc, g):
    return NG * qc + g


def wait(eng, sem, value):
    if not isinstance(value, int) or value > 0:
        eng.wait_ge(sem, value)


def wait_apart(eng, sem, value, true_sem, true_value):
    wait(eng, sem, value)
    eng.wait_ge(true_sem, true_value)


def layernorm_projections(nc, io, scratch, first_loads, rest_out):
    parts_d, v_d, rest_d = scratch
    with ExitStack() as ctx:
        def sb(name, shape, dt=F32):
            return ctx.enter_context(nc.sbuf_tensor(name, shape, dt))

        def sem(name):
            return ctx.enter_context(nc.semaphore(name))

        x_sb = sb("x_sb", [P, NCH * NT, C])
        xn = sb("xn", [P, 2, NT, C])
        xs = sb("xs", [P, 2, 2, CH])
        xnT = sb("xnT", [P, 2, T])
        wqkv = sb("wqkv", [P, 2, 3 * C])
        wbase = sb("wbase", [P, 2, C])
        ident = sb("ident", [P, P])
        stats = sb("stats", [P, NT, 6])
        mv = sb("mv", [P, NT, 2])
        var = sb("var", [P, NT])
        std = sb("std", [P, NT])
        rs = sb("rs", [P, NT])
        tq = sb("tq", [P, NT])
        ts2 = sb("ts2", [P, NT])
        th = sb("th", [P, NT])
        rstd = sb("rstd", [P, NT])
        sum1 = sb("sum1", [P, 2, NCH])
        sum2 = sb("sum2", [P, 2, NCH])
        junk = sb("junk", [P, 2, CH], BF16)
        stage = sb("stage", [P, 4, 3, CH], BF16)
        rest1 = sb("rest1", [P, 2, CH])
        vst = sb("vst", [P, 2, NG, NT, J * D])
        muT = sb("muT", [P, 2, E])
        sgT = sb("sgT", [P, 2, E])
        sq = sb("sq", [P, 2, E])
        iv = sb("iv", [P, 2, E])
        miv = sb("miv", [P, 2, E])
        m2iv = sb("m2iv", [P, 2, E])
        mmiv = sb("mmiv", [P, 2, E])
        ones = sb("ones", [P, 1])
        m1 = sb("m1", [P, 2])
        m2 = sb("m2", [P, 2])
        m1s = sb("m1s", [P, 2])
        m2s = sb("m2s", [P, 2])
        nloss = sb("nloss", [1, E])
        best = sb("best", [1, 8])
        index = sb("index", [1, 8], U32)
        wdown = sb("wdown", [P, 2, R])
        bdown = sb("bdown", [R, 1])
        wup = sb("wup", [P, 2, R + 1])
        wconv = sb("wconv", [P, 2, C])
        brow = sb("brow", [R + 1, C])
        bbase = sb("bbase", [R + 1, C])
        wuc0 = sb("wuc0", [R + 1, C])
        wuc = sb("wuc", [R + 1, C])
        hT = sb("hT", [R + 1, 2, CH])

        tp = ctx.enter_context(nc.psum_tensor("tp", [P, 2, CH], F32))
        qk_ps = ctx.enter_context(nc.psum_tensor("qk_ps", [P, 2, CH], F32))
        vb_ps = ctx.enter_context(nc.psum_tensor("vb_ps", [P, 4, CH], F32))

        x_in = [sem(f"x_in{n}") for n in range(2)]
        w_in = sem("w_in")
        ln_step = sem("ln_step")
        var_ready = sem("var_ready")
        std_ready = sem("std_ready")
        xn_ready = sem("xn_ready")
        tp_ready = sem("tp_ready")
        tp_copied = sem("tp_copied")
        tp_squared = sem("tp_squared")
        qk_ready = sem("qk_ready")
        part1_ready = sem("part1_ready")
        rest_ready = sem("rest_ready")
        part2_ready = sem("part2_ready")
        part3_ready = sem("part3_ready")
        parts_out = [sem(f"parts_out{n}") for n in range(4)]
        v_psum = sem("v_psum")
        v_staged = sem("v_staged")
        v_out = [sem(f"v_out{n}") for n in range(2)]
        base_ready = sem("base_ready")
        base_added = sem("base_added")
        set_up = sem("set_up")
        xnT_ready = sem("xnT_ready")
        mean_ready = sem("mean_ready")
        loss_step = sem("loss_step")
        loss_ready = sem("loss_ready")
        index_ready = sem("index_ready")
        expert_in = sem("expert_in")
        wuc_psum = sem("wuc_psum")
        wuc_ready = sem("wuc_ready")
        h_psum = sem("h_psum")
        h_ready = sem("h_ready")
        ffn_ready = sem("ffn_ready")
        ffn_added = sem("ffn_added")
        block = ctx.enter_context(nc.Block())

        def chunks(eng, body, peeled=False):
            if peeled:
                for c in range(NCH):
                    body(c, c % 2)
                return
            body(0, 0)
            body(1, 1)
            with eng.Fori(1, NCH // 2 - 1) as pair:
                body(pair * 2, 0)
                body(pair * 2 + 1, 1)
            body(NCH - 2, 0)
            body(NCH - 1, 1)

        def x_rows(c):
            return io["x"][c * CH:(c + 1) * CH, :].rearrange("(t p) n -> p t n", p=P)

        W_COUNT = 8

        @block.sync
        def _(sp):
            for c in range(NCH):
                wait(sp, x_in[c % 2], DMA * (c // 2))
                sp.dma_start(x_sb[:, c * NT:(c + 1) * NT, :], x_rows(c)).then_inc(x_in[c % 2], DMA)

            def load_expert():
                sp.wait_ge(index_ready, 1)
                expert = sp.value_load(index[0:1, 0:1], min_val=0, max_val=E - 1)
                sp.dma_start(wdown[:, :, :].rearrange("p a b -> p (a b)"),
                             io["down_W"][bass.ds(expert * P, P), :]).then_inc(expert_in, DMA)
                sp.dma_start(bdown[:, :], io["down_b"][bass.ds(expert * R, R), :]).then_inc(expert_in, DMA)
                sp.dma_start(wup[:, :, :].rearrange("p a b -> p (a b)"),
                             io["up_W"][bass.ds(expert * P, P), :]).then_inc(expert_in, DMA)
                sp.dma_start(wconv[:, :, :].rearrange("p a b -> p (a b)"),
                             io["conv_W"][bass.ds(expert * P, P), :]).then_inc(expert_in, DMA)
                sp.dma_start(brow[R:R + 1, :], io["conv_b"][bass.ds(expert, 1), :]).then_inc(expert_in, DMA)

            def store(c, par):
                for u in range(4):
                    if isinstance(c, int) and c == NCH - 1 and u == 0:
                        load_expert()
                    sp.wait_ge(part3_ready, c * 4 + (u + 1))
                    sp.dma_start(
                        parts_d[(u // 2) * 3 * C:(u // 2 + 1) * 3 * C, bass.ds(c * CH, CH)]
                        .rearrange("(s n) t -> n s t", s=3)[(u % 2) * P:(u % 2 + 1) * P],
                        stage[:, u, :, :]).then_inc(parts_out[u], DMA)
                sp.wait_ge(v_staged, c * NT + NT)
                sp.dma_start(v_d.rearrange("(g p) n -> p g n", p=P)[:, :, bass.ds(c * 256, 256)],
                             vst[:, par, :, :, :].rearrange("p g t n -> p g (t n)")).then_inc(v_out[par], DMA)

            chunks(sp, store)
            def store_rest(c, par):
                sp.wait_ge(ffn_added, c * NT + NT)
                sp.dma_start(rest_d[bass.ds(c * CH, CH), :].rearrange("(t p) n -> p t n", p=P),
                             x_sb[:, bass.ds(c * NT, NT), :]).then_inc(rest_out, DMA)

            for u in range(4):
                sp.wait_ge(parts_out[u], DMA * NCH)
            for n in range(2):
                sp.wait_ge(v_out[n], DMA * NCH // 2)
            first_loads(sp)
            chunks(sp, store_rest)

        @block.scalar
        def _(act):
            act.dma_start(ident[:, :], io["identity"]).then_inc(w_in, DMA)
            act.dma_start(wqkv[:, :, :], io["w_qkv"].rearrange("(a p) n -> p a n", p=P)).then_inc(w_in, DMA)
            act.dma_start(wbase[:, :, :], io["base_W"].rearrange("(a p) n -> p a n", p=P)).then_inc(w_in, DMA)
            act.dma_start(muT[:, :, :], io["disc_mu"].rearrange("(a p) n -> p a n", p=P)).then_inc(w_in, DMA)
            act.dma_start(sgT[:, :, :], io["disc_sigma"].rearrange("(a p) n -> p a n", p=P)).then_inc(w_in, DMA)
            act.wait_ge(set_up, 1)
            act.dma_start(bbase[R:R + 1, :], io["base_b"]).then_inc(w_in, DMA)

            def root(c):
                act.wait_ge(var_ready, c + 1)
                nc.scalar.activation(std[:, :], var[:, :], ACT.Sqrt).then_inc(std_ready, 1)

            def take_transposed(c, par):
                for h in range(2):
                    act.wait_ge(tp_ready, c * 2 + (h + 1))
                    if not isinstance(c, int) or c >= 2:
                        act.wait_ge(base_ready, (c - 1) * NT)
                        act.wait_ge(xnT_ready, c - 1)
                    nc.scalar.activation(xs[:, par, h, :], tp[:, h, :], ACT.Copy,
                                         accum_out=sum1[:, h, bass.ds(c, 1)]).then_inc(tp_copied, 1)
                    wait(act, tp_squared, c * 2 + (h - 1))
                    nc.scalar.activation(junk[:, h, :], tp[:, h, :], ACT.Square,
                                         accum_out=sum2[:, h, bass.ds(c, 1)]).then_inc(tp_squared, 1)

            root(0)
            root(1)
            take_transposed(0, 0)

            def body(c, par):
                if not isinstance(c, int) or c + 2 < NCH:
                    root(c + 2)
                if not isinstance(c, int) or c + 1 < NCH:
                    take_transposed(c + 1, 1 - par)
                for u in range(4):
                    act.wait_ge(qk_ready, c * 4 + (u + 1))
                    wait(act, parts_out[u], c * DMA)
                    nc.scalar.activation(stage[:, u, 0, :], qk_ps[:, u % 2, :], ACT.Copy).then_inc(part1_ready, 1)
                for t in range(NT):
                    act.wait_ge(v_psum, c * NT + (t + 1))
                    if t == 0 and (not isinstance(c, int) or c >= 2):
                        act.wait_ge(v_out[par], (c - par) * (DMA // 2))
                    nc.scalar.activation(vst[:, par, :, t, :],
                                         vb_ps[:, t % 2, 0:C].rearrange("p (g n) -> p g n", g=NG),
                                         ACT.Copy).then_inc(v_staged, 1)

            chunks(act, body)

        @block.gpsimd
        def _(pool):
            def body(c, par):
                pool.wait_ge(tp_copied, c * 2 + 2)
                nc.gpsimd.tensor_copy(xnT[:, :, bass.ds(c * CH, CH)], xs[:, par, :, :]).then_inc(xnT_ready, 1)
                for u in range(4):
                    n = c * 4 + u
                    wait(pool, parts_out[u], c * DMA)
                    pool.wait_ge(part2_ready, n + 1)
                    nc.gpsimd.tensor_tensor(stage[:, u, 2, :], rest1[:, u % 2, :], stage[:, u, 1, :],
                                            ALU.subtract).then_inc(part3_ready, 1)

            chunks(pool, body, peeled=True)

        @block.vector
        def _(dve):
            v = nc.vector
            v.memset(brow[:, :], 0.0)
            v.memset(ones[:, :], 1.0)
            v.memset(hT[R:R + 1, :, :], 1.0)
            v.memset(bbase[:, :], 0.0).then_inc(set_up, 1)
            LN_STEPS = 7

            def layernorm(c, par):
                step = [0]

                def link(ins):
                    step[0] += 1
                    ins.then_inc(ln_step, 1)
                    dve.wait_ge(ln_step, c * LN_STEPS + step[0])

                dve.wait_ge(x_in[par], (c - par) * (DMA // 2) + DMA)
                wait(dve, xn_ready, c)
                for t in range(NT):
                    last = v.bn_stats(stats[:, t, :], x_sb[:, bass.ds(c * NT + t, 1), :]
                                      .rearrange("p a n -> p (a n)"))
                link(last)
                for t in range(NT):
                    last = v.bn_aggr(mv[:, t, :], stats[:, t, :])
                link(last)
                v.tensor_scalar(var[:, :], mv[:, :, 1], EPS, None, ALU.add).then_inc(var_ready, 1)
                dve.wait_ge(std_ready, c + 1)
                link(v.reciprocal(rs[:, :], std[:, :]))
                link(v.tensor_tensor(tq[:, :], var[:, :], rs[:, :], ALU.mult))
                link(v.tensor_tensor(ts2[:, :], tq[:, :], std[:, :], ALU.add))
                link(v.tensor_scalar(th[:, :], ts2[:, :], 0.5, None, ALU.mult))
                link(v.reciprocal(rstd[:, :], th[:, :]))
                assert step[0] == LN_STEPS
                if not isinstance(c, int) or c >= 2:
                    dve.wait_ge(tp_ready, (c - 1) * 2)
                for t in range(NT):
                    last = v.tensor_scalar(xn[:, par, t, :], x_sb[:, bass.ds(c * NT + t, 1), :]
                                           .rearrange("p a n -> p (a n)"),
                                           mv[:, t, 0:1], rstd[:, t:t + 1], ALU.subtract, ALU.mult)
                last.then_inc(xn_ready, 1)

            layernorm(0, 0)
            layernorm(1, 1)

            def body(c, par):
                if c + 2 < NCH:
                    layernorm(c + 2, par)
                for u in range(4):
                    n = c * 4 + u
                    dve.wait_ge(part1_ready, n + 1)
                    wait(dve, part3_ready, n - 1)
                    v.tensor_tensor(rest1[:, u % 2, :], qk_ps[:, u % 2, :], stage[:, u, 0, :],
                                    ALU.subtract).then_inc(rest_ready, 1)
                    wait(dve, parts_out[u], c * DMA)
                    dve.wait_ge(rest_ready, n + 1)
                    v.tensor_copy(stage[:, u, 1, :], rest1[:, u % 2, :]).then_inc(part2_ready, 1)
                for t in range(NT):
                    dve.wait_ge(base_ready, c * NT + (t + 1))
                    xt = x_sb[:, bass.ds(c * NT + t, 1), :].rearrange("p a n -> p (a n)")
                    v.tensor_tensor(xt, vb_ps[:, 2 + t % 2, 0:C], xt, ALU.add).then_inc(base_added, 1)

            done = [0]

            def link(ins):
                done[0] += 1
                ins.then_inc(loss_step, 1)
                dve.wait_ge(loss_step, done[0])

            dve.wait_ge(w_in, DMA * 6)
            link(v.tensor_tensor(sq[:, :, :], sgT[:, :, :], sgT[:, :, :], ALU.mult))
            link(v.reciprocal(iv[:, :, :], sq[:, :, :]))
            link(v.tensor_tensor(miv[:, :, :], muT[:, :, :], iv[:, :, :], ALU.mult))
            link(v.tensor_scalar(m2iv[:, :, :], miv[:, :, :], -2.0, None, ALU.mult))
            link(v.tensor_tensor(mmiv[:, :, :], miv[:, :, :], muT[:, :, :], ALU.mult))

            def means():
                dve.wait_ge(tp_squared, 2 * NCH)
                link(v.tensor_reduce(out=m1s[:, :], in_=sum1[:, :, :], axis=AX.X, op=ALU.add))
                link(v.tensor_reduce(out=m2s[:, :], in_=sum2[:, :, :], axis=AX.X, op=ALU.add))
                link(v.tensor_scalar(m1[:, :], m1s[:, :], 1.0 / T, None, ALU.mult))
                v.tensor_scalar(m2[:, :], m2s[:, :], 1.0 / T, None, ALU.mult).then_inc(mean_ready, 1)

            def choose():
                dve.wait_ge(loss_ready, 1)
                link(v.tensor_scalar(nloss[:, :], tp[0:1, 0, 0:E], -1.0 / C, None, ALU.mult))
                link(v.max(best[:, :], nloss[:, :]))
                v.max_index(index[:, :], best[:, :], nloss[:, :]).then_inc(index_ready, 1)

            for c in range(NCH):
                body(c, c % 2)
                if c == NCH - 2:
                    means()
                    choose()
            dve.wait_ge(wuc_psum, 1)
            link(v.tensor_tensor(wuc0[:, :], tp[0:R + 1, 1, 0:C], brow[:, :], ALU.add))
            v.tensor_tensor(wuc[:, :], wuc0[:, :], bbase[:, :], ALU.add).then_inc(wuc_ready, 1)

            def hidden(c, par):
                dve.wait_ge(h_psum, c + 1)
                if c >= 2:
                    dve.wait_ge(ffn_ready, (c - 1) * NT)
                v.tensor_scalar(hT[0:R, par, :], qk_ps[0:R, par, :], bdown[:, 0:1], 0.0,
                                ALU.add, ALU.max).then_inc(h_ready, 1)

            def ffn(c, par):
                if c + 1 < NCH:
                    hidden(c + 1, 1 - par)
                for t in range(NT):
                    dve.wait_ge(ffn_ready, c * NT + (t + 1))
                    xt = x_sb[:, bass.ds(c * NT + t, 1), :].rearrange("p a n -> p (a n)")
                    v.tensor_tensor(xt, vb_ps[:, t, 0:C], xt, ALU.add).then_inc(ffn_added, 1)

            dve.wait_ge(base_added, NT * NCH)
            hidden(0, 0)
            chunks(dve, ffn, peeled=True)

        @block.tensor
        def _(pe):
            pe.wait_ge(w_in, DMA * 6)

            def transpose(c, par):
                pe.wait_ge(xn_ready, c + 1)
                for h in range(2):
                    wait(pe, tp_squared, c * 2 - 1 + h)
                    for t in range(NT):
                        last = nc.tensor.transpose(tp[:, h, t * P:(t + 1) * P],
                                                   xn[:, par, t, h * P:(h + 1) * P], ident[:, :])
                    last.then_inc(tp_ready, 1)

            def choose():
                pe.wait_ge(mean_ready, 1)
                terms = [(m2[:, h:h + 1], iv[:, h, :]) for h in range(2)]
                terms += [(m1[:, h:h + 1], m2iv[:, h, :]) for h in range(2)]
                terms += [(ones[:, :], mmiv[:, h, :]) for h in range(2)]
                for n, (a, b) in enumerate(terms):
                    last = nc.tensor.matmul(tp[0:1, 0, 0:E], a, b, start=(n == 0), stop=(n == len(terms) - 1))
                last.then_inc(loss_ready, 1)

            transpose(0, 0)

            def body(c, par):
                if not isinstance(c, int) or c + 1 < NCH:
                    transpose(c + 1, 1 - par)
                else:
                    choose()
                pe.wait_ge(tp_copied, c * 2 + 2)
                for u in range(4):
                    n = c * 4 + u
                    wait(pe, rest_ready, n - 1)
                    for h in range(2):
                        last = nc.tensor.matmul(qk_ps[:, u % 2, :], wqkv[:, h, u * P:(u + 1) * P],
                                                xs[:, par, h, :], start=(h == 0), stop=(h == 1))
                    last.then_inc(qk_ready, 1)
                for t in range(NT):
                    wait(pe, v_staged, c * NT + (t - 1))
                    for h in range(2):
                        last = nc.tensor.matmul(vb_ps[:, t % 2, 0:C], xs[:, par, h, t * P:(t + 1) * P],
                                                wqkv[:, h, 2 * C:3 * C], start=(h == 0), stop=(h == 1))
                    last.then_inc(v_psum, 1)
                    wait(pe, base_added, c * NT + (t - 1))
                    for h in range(2):
                        last = nc.tensor.matmul(vb_ps[:, 2 + t % 2, 0:C], xs[:, par, h, t * P:(t + 1) * P],
                                                wbase[:, h, :], start=(h == 0), stop=(h == 1))
                    last.then_inc(base_ready, 1)

            chunks(pe, body)
            pe.wait_ge(expert_in, DMA * 5)
            for h in range(2):
                last = nc.tensor.matmul(tp[0:R + 1, 1, 0:C], wup[:, h, :], wconv[:, h, :],
                                        start=(h == 0), stop=(h == 1))
            last.then_inc(wuc_psum, 1)
            pe.wait_ge(xnT_ready, NCH)
            pe.wait_ge(v_staged, NCH * NT)
            pe.wait_ge(base_added, NCH * NT)
            pe.wait_ge(rest_ready, NCH * 4)
            pe.wait_ge(wuc_ready, 1)

            def hidden(c, par):
                wait(pe, h_ready, c - 1)
                for h in range(2):
                    last = nc.tensor.matmul(qk_ps[0:R, par, :], wdown[:, h, :],
                                            xnT[:, h, bass.ds(c * CH, CH)], start=(h == 0), stop=(h == 1))
                last.then_inc(h_psum, 1)

            def ffn(c, par):
                if not isinstance(c, int) or c + 1 < NCH:
                    hidden(c + 1, 1 - par)
                pe.wait_ge(h_ready, c + 1)
                for t in range(NT):
                    wait(pe, ffn_added, c * NT + (t - 3))
                    nc.tensor.matmul(vb_ps[:, t, 0:C], hT[:, par, t * P:(t + 1) * P], wuc[:, :],
                                     start=True, stop=True).then_inc(ffn_ready, 1)

            hidden(0, 0)
            chunks(pe, ffn)


class FirstLoads:

    def __init__(self, nc, ctx, io, scratch):
        def sb(name, shape, dt=F32):
            return ctx.enter_context(nc.sbuf_tensor(name, shape, dt))

        self.io, (self.parts_d, self.v_d, _) = io, scratch
        self.k_0 = sb("k_0", [P, HEADS * CH], BF16)
        self.q_st = sb("q_st", [P, NG * J * CH], BF16)
        self.v_buf = sb("v_buf", [P, 2 * NCH * NT * J * D])
        self.w_out = sb("w_out", [P, NP, C])
        self.ident = sb("ident_b", [P, P], BF16)
        self.mask = sb("mask", [P, CH], BF16)
        self.k_in, self.q_in, self.v_in, self.const_in, self.rest_out = (
            ctx.enter_context(nc.semaphore(n)) for n in ("k_in", "q_in", "v_in", "const_in", "rest_out"))

    def load_k(self, sp, c, into):
        wait(sp, self.k_in, c * K_COUNT)
        kv = into.rearrange("p (h t) -> p h t", h=HEADS)
        for n, (_, part) in enumerate(PRODUCTS):
            src = self.parts_d[(3 + part) * C:(4 + part) * C, c * CH:(c + 1) * CH]
            sp.dma_start(kv[n * D:(n + 1) * D], src.rearrange("(h d) t -> d h t", d=D)).then_inc(self.k_in, DMA)
        sp.dma_start(kv[SK:SM], self.io["head_rows"].rearrange("r (h t) -> r h t", h=HEADS))\
          .then_inc(self.k_in, DMA)

    def load_q(self, sp, n, qc, g):
        wait(sp, self.q_in, n * Q_COUNT)
        for r, (part, _) in enumerate(PRODUCTS):
            src = self.parts_d[part * C + g * J * D:part * C + (g + 1) * J * D, qc * CH:(qc + 1) * CH]
            sp.dma_start(self.q_st[r * D:(r + 1) * D, g * J * CH:(g + 1) * J * CH]
                         .rearrange("p (j t) -> p j t", j=J),
                         src.rearrange("(j d) t -> d j t", d=D)).then_inc(self.q_in, DMA)

    def load_v(self, sp, n, g, count):
        wait(sp, self.v_in, n * DMA)
        sp.dma_start(self.v_buf[:, (n % 2) * NCH * 256:(n % 2) * NCH * 256 + count * 256],
                     self.v_d[g * P:(g + 1) * P, 0:count * 256]).then_inc(self.v_in, DMA)

    def start(self, sp):
        self.load_k(sp, 0, self.k_0[:, :])
        for g in range(3):
            self.load_q(sp, g, 0, g)
        self.load_v(sp, 0, 0, 1)
        sp.dma_start(self.ident[:, :], self.io["identity_b"]).then_inc(self.const_in, DMA)
        sp.dma_start(self.mask[:, :], self.io["mask"]).then_inc(self.const_in, DMA)
        sp.dma_start(self.w_out[:, :, :], self.io["w_out"].rearrange("(g p) n -> p g n", p=P))\
          .then_inc(self.const_in, DMA)


def attention(nc, io, scratch, out, loads):
    parts_d, v_d, rest_d = scratch
    with ExitStack() as ctx:
        def sb(name, shape, dt=F32):
            return ctx.enter_context(nc.sbuf_tensor(name, shape, dt))

        def sem(name):
            return ctx.enter_context(nc.semaphore(name))

        q_st, v_buf, k_0 = loads.q_st, loads.v_buf, loads.k_0
        k_in, q_in, v_in = loads.k_in, loads.q_in, loads.v_in
        w_out, ident, mask, const_in = loads.w_out, loads.ident, loads.mask, loads.const_in
        k_st = sb("k_st", [P, (NCH - 1) * HEADS * CH], BF16)
        v_ring = sb("v_ring", [P, NT, J, 32])
        probs = sb("probs", [P, 2, J, CH])
        on = sb("on", [P, (NP + 1) * CH])
        o_pair = sb("o_pair", [P, CH])
        o_t = sb("o_t", [P, CH])
        l_rec = sb("l_rec", [P, CH // 32])
        rest = sb("rest", [P, NT, C])
        masked = sb("masked", [P, 2, CH], BF16)
        maxes = sb("maxes", [P, NCH + 1, NT * J])
        negmax = sb("negmax", [P, NT * J])
        negrest = sb("negrest", [P, NT * J])
        mparts = sb("mparts", [P, NT, P], BF16)

        s1 = ctx.enter_context(nc.psum_tensor("s1", [P, 4, CH], F32))
        s2 = ctx.enter_context(nc.psum_tensor("s2", [P, 2, CH], F32))
        acc = ctx.enter_context(nc.psum_tensor("acc", [P, CH], F32))
        mt_ps = ctx.enter_context(nc.psum_tensor("mt_ps", [P, 2 * CH], BF16))

        proj_ps = mt_ps[:, 0:2 * C].bitcast(F32)

        set_up = sem("set_up2")
        rest_in = sem("rest_in")
        s1_ready = sem("s1_ready")
        s1_read = sem("s1_read")
        split_step = sem("split_step")
        m_ready = sem("m_ready")
        mt_ready = sem("mt_ready")
        m_placed = sem("m_placed")
        s2_ready = sem("s2_ready")
        exp_done = sem("exp_done")
        mask_done = sem("mask_done")
        v_ready = sem("v_ready")
        av_done = sem("av_done")
        acc_read = sem("acc_read")
        l_ready = sem("l_ready")
        scaled = sem("scaled")
        on_ready = sem("on_ready")
        proj_ready = sem("proj_ready")
        proj_added = sem("proj_added")
        out_done = sem("out_done")
        block = ctx.enter_context(nc.Block())

        SPLIT_STEPS = 4

        def k_at(rows, g, j, kc, at, n):
            if isinstance(kc, int) and kc == 0:
                return k_0[0:rows, bass.ds((g * J + j) * CH + at, n)]
            return k_st[0:rows, bass.ds((kc - 1) * (HEADS * CH) + ((g * J + j) * CH + at), n)]

        def items(eng, body, peeled=False):
            for qc in range(NCH):
                for half in range(2):
                    if peeled or half == 1 or qc in (0, 1, NCH - 1):
                        for gg in range(2):
                            body(qc, 2 * half + gg, half, gg)
                    else:
                        with eng.Fori(0, 2) as gg:
                            body(qc, gg, half, gg)

        def turns(eng, first, count, body):
            if count - first == 1:
                body(first)
            elif count > first:
                with eng.Fori(first, count) as k:
                    body(k)

        def ahead(qc, half, gg):
            if half == 0:
                return qc, gg + 2
            return (qc + 1, gg) if qc + 1 < NCH else None

        def on_slot(qc, pair):
            return qc % 2 if pair == 0 else 2

        SPREAD = (((1, 1, 2, 1), (0, 0, 0, 0), (1, 1, 1, 0)),
                  ((0, 0, 0, 0), (1, 1, 1, 1), (2, 1, 1, 0)))

        def spread(qc, half, k, i):
            diagonal, first, last = SPREAD[half]
            if qc == 1:
                first, last = (), [m + n for m, n in zip(first, last)]
            if isinstance(k, int) and k == 0:
                before, counts = 0, diagonal
            elif isinstance(k, int) and k == qc:
                before, counts = sum(diagonal) + sum(first), last
            elif isinstance(k, int) and k == 1:
                before, counts = sum(diagonal), first
            else:
                return sum(diagonal) + sum(first), []
            before += sum(counts[:i])
            return before, [divmod(before + m, 2) for m in range(counts[i])]

        def ahead_pairs(qc, half, k, i):
            both = [0, 1]
            if qc == 0:
                if half == 0:
                    return 2 * i, [(None, i, r) for r in both]
                return 4 * i, [(0, i, r) for r in both] + [(None, i, r) for r in both]
            before, some = spread(qc, half, k, i)
            some = [(half, t, r) for t, r in some]
            if isinstance(k, int) and k == 0:
                whole = [(0, i, r) for r in both] if half else []
                return before + (2 * i if half else 0), whole + some
            before = before + 8 * half
            if isinstance(k, int) and k == qc:
                whole = [(None, i, r) for r in both]
                return before + 8 * (k - 1) + 2 * i, some[0:1] + whole + some[1:]
            return (k - 1) * 8 + (before + 2 * i), [(k + half, i, r) for r in both] + some

        def pair_slot(qc, half, k, i):
            return ahead_pairs(qc, half, k if isinstance(k, int) else 2, i)[0] % 2

        def tail(qc, g):
            return isinstance(g, int) and qc == NCH - 1 and g >= 2

        def s2_bank(qc, g, j):
            return s1[:, j, :] if tail(qc, g) else s2[:, j % 2, :]

        @block.sync
        def _(sp):
            sp.wait_ge(loads.rest_out, DMA * NCH)
            loads.load_k(sp, 1, k_st[:, 0:HEADS * CH])

            def body(qc, g, half, gg):
                n = item(qc, g)
                if g == 0 and qc + 2 < NCH:
                    loads.load_k(sp, qc + 2, k_st[:, (qc + 1) * HEADS * CH:(qc + 2) * HEADS * CH])
                if n + 3 < NCH * NG:
                    wait(sp, s2_ready, micro(qc, g) * 4)
                    loads.load_q(sp, n + 3, *divmod(n + 3, NG))
                if n + 1 < NCH * NG:
                    wait(sp, v_ready, micro(qc, g))
                    loads.load_v(sp, n + 1, (n + 1) % NG, (n + 1) // NG + 1)
                if g == 1 and qc > 0:
                    load_rest(qc - 1)
                if g == 2 and qc > 0:
                    store(qc - 1)

            def load_rest(c):
                wait(sp, out_done, c * NT * DMA)
                sp.dma_start(rest[:, :, :], rest_d[c * CH:(c + 1) * CH, :]
                             .rearrange("(t p) n -> p t n", p=P)).then_inc(rest_in, DMA)

            def store(c):
                for t in range(NT):
                    sp.wait_ge(proj_added, c * NT + t + 1)
                    sp.dma_start(out[c * CH + t * P:c * CH + (t + 1) * P, :],
                                 rest[:, t, :]).then_inc(out_done, DMA)

            items(sp, body, peeled=True)
            load_rest(NCH - 1)
            store(NCH - 1)
            sp.wait_ge(out_done, NCH * NT * DMA)

        @block.tensor
        def _(pe):
            mm = nc.tensor.matmul

            def max_scores(qc, g, pair, slot, kc, t, r):
                n = P * (t + 1) if kc is None else CH
                wait(pe, s1_read, micro(qc, g) * 2 + pair - 1)
                for j in (2 * r, 2 * r + 1):
                    last = mm(s1[:, 2 * slot + j % 2, 0:n], q_st[0:SK, bass.ds(g * (J * CH) + (j * CH + t * P), P)],
                              k_at(SK, g, j, qc if kc is None else kc, 0, n), start=True, stop=True)
                last.then_inc(s1_ready, 1)

            def scores(qc, g, pos, kc, i, j):
                q0 = i * P if kc is None else 0
                if tail(qc, g):
                    wait(pe, exp_done, micro(qc, g, pos) * 4 + (j - 3))
                else:
                    wait(pe, exp_done, micro(qc, g, pos) * 4 + (j - 1))
                mm(s2_bank(qc, g, j)[:, q0:CH], k_at(SM, g, j, qc if kc is None else kc, i * P, P),
                   q_st[0:SM, bass.ds(g * (J * CH) + (j * CH + q0), CH - q0)],
                   start=True, stop=True).then_inc(s2_ready, 1)

            def weigh(mu, i, diagonal, masks, first, final, taken):
                q0 = i * P if diagonal else 0
                if diagonal:
                    pe.wait_ge(mask_done, masks)
                pe.wait_ge(v_ready, mu + 1)
                if first:
                    wait(pe, acc_read, taken)
                for j in range(J):
                    last = mm(acc[32 * j:32 * j + 32, q0:CH], v_ring[:, i, j, :], probs[:, i % 2, j, q0:CH],
                              start=first, stop=final, tile_position=(0, 32 * j))
                last.then_inc(av_done, 1)

            def transpose_maxima(n, projected):
                pe.wait_ge(m_ready, n + 1)
                wait(pe, m_placed, n * J)
                wait(pe, proj_added, projected * NT)
                for t in range(NT):
                    last = nc.tensor.transpose(mt_ps[:, t * P:(t + 1) * P], mparts[:, t, :], ident[:, :])
                last.then_inc(mt_ready, 1)

            def step(qc, g, pos, kc, i, pairs, late):
                for j in range(J):
                    scores(qc, g, pos, kc, i, j)
                    if j == 1:
                        for pair in pairs[0:2]:
                            max_scores(*pair)
                late()
                for pair in pairs[2:]:
                    max_scores(*pair)

            def project(c, t):
                if t == 0:
                    pe.wait_ge(on_ready, (c + 1) * NP)
                    pe.wait_ge(m_placed, min((c + 2) * NG, NCH * NG) * J)
                wait(pe, proj_added, c * NT + t)
                for pair in range(NP):
                    at = on_slot(c, pair) * CH + t * P
                    last = mm(proj_ps, on[:, at:at + P],
                              w_out[:, pair, :], start=(pair == 0), stop=(pair == NP - 1))
                last.then_inc(proj_ready, 1)

            pe.wait_ge(const_in, DMA * 3)
            pe.wait_ge(k_in, K_COUNT)
            for g in range(2):
                pe.wait_ge(q_in, (g + 1) * Q_COUNT)
                for t in range(NT):
                    for r in range(2):
                        max_scores(0, g, 2 * t + r, r, None, t, r)
            transpose_maxima(0, 0)

            def body(qc, g, half, gg):
                n = item(qc, g)
                start = micro(qc, g)
                nxt = ahead(qc, half, gg)
                masks = n * NT
                final = n + 1 == NCH * NG
                if nxt:
                    pe.wait_ge(q_in, (n + 3) * Q_COUNT)
                    if half == 1:
                        pe.wait_ge(k_in, (qc + 2) * K_COUNT)
                pe.wait_ge(m_placed, (n + 1) * J)
                if tail(qc, g):
                    pe.wait_ge(s1_read, micro(NCH, 0) * 2)

                def pairs(k, i):
                    if not nxt:
                        return []
                    first, work = ahead_pairs(qc, half, k, i)
                    slot = pair_slot(qc, half, k, i)
                    return [(*nxt, first + m, (slot + m) % 2, *w) for m, w in enumerate(work)]

                for i in range(NT):
                    def late():
                        if i:
                            weigh(start + (i - 1), i - 1, True, masks + i, i == 1, False, n)
                        elif n:
                            weigh(start - 1, NT - 1, n <= NG, masks, False, True, None)
                    step(qc, g, i, None, i, pairs(0, i), late)
                    if i == 1 and not final:
                        transpose_maxima(n + 1, max(0, qc - (g <= 2)))

                def full(k):
                    pos = k * NT
                    first = isinstance(k, int) and k == 1
                    for i in range(NT):
                        def late():
                            if i == 0 and first:
                                weigh(start + (NT - 1), NT - 1, True, masks + NT, False, False, None)
                            else:
                                weigh(start + (pos + (i - 1)), (i - 1) % NT, False, None, False, False, None)
                        step(qc, g, pos + i, k - 1, i, pairs(k, i), late)
                        if first and g == 2:
                            project(qc - 1, i)

                if qc:
                    full(1)
                turns(pe, 2, qc, full)
                if qc > 1:
                    full(qc)

            items(pe, body, peeled=True)
            pe.wait_ge(exp_done, micro(NCH, 0) * 4)
            weigh(micro(NCH, 0) - 1, NT - 1, False, None, False, True, None)
            for t in range(NT):
                project(NCH - 1, t)

        @block.scalar
        def _(act):
            def place_maxima(n, slot, j):
                act.wait_ge(mt_ready, n + 1)
                nc.scalar.activation(q_st[SK:SM, bass.ds(slot * (J * CH) + j * CH, CH)], mt_ps[SK:SM, 0:CH],
                                     ACT.Copy).then_inc(m_placed, 1)

            def exps(qc, g, pos, q0, i, after):
                mu = micro(qc, g, pos)
                wait(act, av_done, mu - 1)
                for j in range(J):
                    act.wait_ge(s2_ready, mu * 4 + (j + 1))
                    nc.scalar.activation(probs[:, i % 2, j, q0:CH], s2_bank(qc, g, j)[:, q0:CH], ACT.Exp,
                                         scale=SCALE).then_inc(exp_done, 1)
                    after(j)

            for j in range(J):
                place_maxima(0, 0, j)

            def body(qc, g, half, gg):
                n = item(qc, g)
                for i in range(NT):
                    def after(j):
                        if i >= 2 and j % 2 == 1 and not (isinstance(n, int) and n + 1 == NCH * NG):
                            place_maxima(n + 1, gg + 1 if half == 0 else gg * -3 + 3, 2 * (i - 2) + j // 2)
                    exps(qc, g, i, i * P, i, after)

                def full(kc):
                    for i in range(NT):
                        exps(qc, g, kc * NT + (NT + i), 0, i, lambda j: None)
                turns(act, 0, qc, full)

            items(act, body)

        @block.gpsimd
        def _(pool):
            nc.gpsimd.memset(v_ring[:, :, :, :], 0.0).then_inc(set_up, 1)
            pool.wait_ge(set_up, 1)
            nc.gpsimd.memset(v_ring[:, :, :, D:D + 1], 1.0).then_inc(set_up, 1)
            nc.gpsimd.memset(mparts[:, :, :], 0.0).then_inc(set_up, 1)
            pool.wait_ge(set_up, 3)

            def place_v(qc, g, gg, pos, at, i):
                mu = micro(qc, g, pos)
                wait_apart(pool, av_done, mu - 3, set_up, 3)
                nc.gpsimd.tensor_copy(v_ring[:, i, :, 0:D],
                                      v_buf[:, bass.ds(gg * (NCH * 256) + at, J * D)]
                                      .rearrange("p (j d) -> p j d", j=J)).then_inc(v_ready, 1)

            def normalise(n):
                pool.wait_ge(l_ready, n)
                wait(pool, on_ready, (n - 1) // 2)
                half = (n - 1) % 2
                dst = o_pair[:, :].rearrange("p (b h d) -> p b h d", h=2, d=D)[:, :, half, :]
                o = o_t[:, :].rearrange("p (b c) -> p b c", c=32)[:, :, 0:D]
                nc.gpsimd.tensor_tensor(dst, o, l_rec[:, :].unsqueeze(2).broadcast_to([P, CH // 32, D]),
                                        ALU.mult).then_inc(scaled, 1)

            def body(qc, g, half, gg):
                n = item(qc, g)
                pool.wait_ge(v_in, (n + 1) * DMA)

                def place(k, i):
                    kc = qc if isinstance(k, int) and k == 0 else k - 1
                    place_v(qc, g, gg, k * NT + i, kc * 256 + i * (J * D), i)

                steps = [(k, i) for k in range(2 if qc else 1) for i in range(NT)]
                for k, i in steps[0:2]:
                    place(k, i)
                for i in range(NT):
                    pool.wait_ge(exp_done, micro(qc, g, i) * 4 + 4)
                    sq = probs[:, i % 2, :, i * P:(i + 1) * P]
                    nc.gpsimd.affine_select(out=sq, in_=sq, compare_op=ALU.is_ge, fill=0.0, base=0,
                                            pattern=[[0, J], [1, P]], channel_multiplier=-1)\
                        .then_inc(mask_done, 1)
                    for s in steps[i + 2:i + 3]:
                        place(*s)
                    if i == 2 and n:
                        normalise(n)
                for s in steps[NT + 2:]:
                    place(*s)

                def full(k):
                    for i in range(NT):
                        place(k, i)
                turns(pool, 2, qc + 1, full)

            items(pool, body, peeled=True)
            normalise(NCH * NG)

        @block.vector
        def _(dve):
            v = nc.vector

            def reduce_pair(qc, g, pair, slot, kc, t, r):
                pair = micro(qc, g) * 2 + pair
                dve.wait_ge(s1_ready, pair + 1)
                if kc is None:
                    n = P * (t + 1)
                    wait(dve, s1_read, pair)
                    for j in (2 * r, 2 * r + 1):
                        last = v.tensor_tensor_reduce(
                            out=masked[:, j % 2, 0:n], in0=s1[:, 2 * slot + j % 2, 0:n], in1=mask[:, CH - n:CH], scale=1.0,
                            scalar=NEG, op0=ALU.add, op1=ALU.max, accum_out=maxes[:, 0, t * J + j:t * J + j + 1])
                else:
                    dst = maxes[:, bass.ds(kc + 1, 1), t * J + 2 * r:t * J + 2 * r + 2].rearrange("p a b -> p (a b)")
                    last = v.tensor_reduce(out=dst, in_=s1[:, 2 * slot:2 * slot + 2, :], axis=AX.X, op=ALU.max)
                last.then_inc(s1_read, 1)

            def split_maxima(qc, g):
                n = item(qc, g)
                done = [0]

                def link(ins):
                    done[0] += 1
                    ins.then_inc(split_step, 1)
                    dve.wait_ge(split_step, n * SPLIT_STEPS + done[0])

                dve.wait_ge(s1_read, (micro(qc, g) + NT * (qc + 1)) * 2)
                wait(dve, m_ready, n)
                link(v.tensor_reduce(out=negmax[:, :], in_=maxes[:, 0:qc + 1, :].rearrange("p k c -> p c k"),
                                     axis=AX.X, op=ALU.max, negate=True))
                wait(dve, mt_ready, n)
                part = mparts[:, :, SK:SM].rearrange("p t (j r) -> p t j r", r=3)
                full = negmax[:, :].rearrange("p (t j) -> p t j", j=J)
                left = negrest[:, :].rearrange("p (t j) -> p t j", j=J)
                link(v.tensor_copy(part[:, :, :, 0], full))
                link(v.tensor_tensor(left, full, part[:, :, :, 0], ALU.subtract))
                link(v.tensor_copy(part[:, :, :, 1], left))
                v.tensor_tensor(part[:, :, :, 2], left, part[:, :, :, 1], ALU.subtract).then_inc(m_ready, 1)
                assert done[0] == SPLIT_STEPS

            def take_acc(n, start):
                dve.wait_ge(av_done, start)
                wait(dve, scaled, n - 1)
                v.transpose(o_t[:, :], acc[:, :]).then_inc(acc_read, 1)

            def invert_sums(n):
                dve.wait_ge(acc_read, n)
                v.reciprocal(l_rec[:, :], o_t[:, :].rearrange("p (b c) -> p b c", c=32)[:, :, D]).then_inc(l_ready, 1)

            def put_back(n):
                qc, pair = divmod(n // 2 - 1, NP)
                slot = on_slot(qc, pair)
                dve.wait_ge(scaled, n)
                wait(dve, proj_ready, (qc - 1 if pair == 0 else qc) * NT)
                v.transpose(on[:, slot * CH:(slot + 1) * CH], o_pair[:, :]).then_inc(on_ready, 1)

            dve.wait_ge(set_up, 3)
            dve.wait_ge(const_in, DMA * 3)
            for g in range(2):
                for t in range(NT):
                    for r in range(2):
                        reduce_pair(0, g, 2 * t + r, r, None, t, r)
                split_maxima(0, g)

            def body(qc, g, half, gg):
                n = item(qc, g)
                nxt = ahead(qc, half, gg)

                def max_step(k, i):
                    if nxt:
                        first, work = ahead_pairs(qc, half, k, i)
                        slot = pair_slot(qc, half, k, i)
                        for m, w in enumerate(work):
                            reduce_pair(*nxt, first + m, (slot + m) % 2, *w)

                for i in range(NT):
                    max_step(0, i)
                    if n:
                        if i == 0:
                            take_acc(n, micro(qc, g))
                        if i == 1:
                            invert_sums(n)
                        if i == 3 and n % 2 == 0:
                            put_back(n)

                def full(k):
                    for i in range(NT):
                        max_step(k, i)
                        if isinstance(k, int) and k == 1 and g == 2:
                            add_projection(qc - 1, i)

                if qc:
                    full(1)
                if nxt:
                    turns(dve, 2, qc, full)
                    if qc > 1:
                        full(qc)
                    split_maxima(*nxt)

            def add_projection(c, t):
                if t == 0:
                    dve.wait_ge(rest_in, (c + 1) * DMA)
                dve.wait_ge(proj_ready, c * NT + t + 1)
                v.tensor_tensor(rest[:, t, :], proj_ps, rest[:, t, :], ALU.add).then_inc(proj_added, 1)

            items(dve, body, peeled=True)
            n = NCH * NG
            take_acc(n, micro(NCH, 0))
            invert_sums(n)
            put_back(n)
            for t in range(NT):
                add_projection(NCH - 1, t)


def build(nc, io, out):
    parts_d = nc.dram_tensor("qk_parts", (6 * C, T), BF16).ap()
    v_d = nc.dram_tensor("v_scratch", (NG * P, NCH * 256), F32).ap()
    rest_d = nc.dram_tensor("rest_scratch", (T, C), F32).ap()
    scratch = (parts_d, v_d, rest_d)
    with ExitStack() as ctx:
        loads = FirstLoads(nc, ctx, io, scratch)
        layernorm_projections(nc, io, scratch, loads.start, loads.rest_out)
        attention(nc, io, scratch, out, loads)


def kernel(**inputs):
    import ml_dtypes
    import numpy as np
    import concourse.bacc as bacc
    from concourse.bass_utils import run_bass_kernel_spmd

    def halves(w):
        return w.reshape(E, 2, P, -1).transpose(0, 2, 1, 3).reshape(E * P, -1)

    a = {k.replace("L0_ffn_", "").replace("L0_attn_", ""): np.asarray(v) for k, v in inputs.items()}
    up = np.concatenate([a["up_W"].transpose(0, 2, 1), a["up_b"][:, :, None]], axis=2)
    w_out = a["w_out"].reshape(NP, 2, J, D, C).transpose(0, 2, 1, 3, 4)
    head_rows = np.repeat(np.eye(J, dtype=ml_dtypes.bfloat16), 3, axis=0)
    head_rows = np.repeat(np.tile(head_rows, (1, NG)), CH, axis=1)
    mask = np.zeros((P, CH), ml_dtypes.bfloat16)
    mask[:, CH - P:][np.triu_indices(P, 1)] = NEG
    arrays = {
        "x": a["x"].reshape(T, C),
        "w_qkv": a["w_qkv"],
        "w_out": w_out.reshape(NP * P, C),
        "base_W": a["base_W"].T,
        "base_b": a["base_b"].reshape(1, C),
        "disc_mu": a["disc_mu"].T,
        "disc_sigma": a["disc_sigma"].T,
        "down_W": halves(a["down_W"]),
        "down_b": a["down_b"].reshape(E * R, 1),
        "up_W": halves(up),
        "conv_W": halves(a["conv_W"].transpose(0, 2, 1)),
        "conv_b": a["conv_b"],
        "identity": np.eye(P, dtype=np.float32),
        "identity_b": np.eye(P, dtype=ml_dtypes.bfloat16),
        "mask": mask,
        "head_rows": head_rows,
    }
    arrays = {k: np.ascontiguousarray(v) for k, v in arrays.items()}
    nc = bacc.Bacc("TRN2", target_bir_lowering=False, num_devices=1)
    io = {k: nc.dram_tensor(f"in_{k}", v.shape, mybir.dt.from_np(v.dtype), kind="ExternalInput").ap()
          for k, v in arrays.items()}
    out = nc.dram_tensor("out_0", (T, C), F32, kind="ExternalOutput").ap()
    build(nc, io, out)
    r = run_bass_kernel_spmd(nc, [{f"in_{k}": v for k, v in arrays.items()}], core_ids=[0])
    return r.results[0]["out_0"].reshape(1, T, C)
```
